# Optimizing a Trainium2 kernel written in Bass

```python
import numpy as np
import jax
import jax.numpy as jnp

def _softmax(x, axis=-1):
    return jax.nn.softmax(x, axis=axis)

def _gelu(x):
    return jax.nn.gelu(x, approximate=True)

def _silu(x):
    return jax.nn.silu(x)

def _sigmoid(x):
    return jax.nn.sigmoid(x)

def _layernorm(x, axis=-1, eps=1e-05):
    m = jnp.mean(x, axis=axis, keepdims=True)
    v = jnp.var(x, axis=axis, keepdims=True)
    return (x - m) / jnp.sqrt(v + eps)

def _scatter_add(tgt, idx, src, axis=0):
    return tgt.at[idx].add(src)

def _segment_sum(src, seg, n):
    return jax.ops.segment_sum(src, seg, n)
kernel_name = 'mk_adaln_d1_jaxref_r4_d39cc9'

def setup_inputs(seed: int=0):
    np.random.seed(seed)
    _w = jnp.asarray

    def _L0_attn_setup():
        import math
        import jax, jax.numpy as jnp
        import numpy as np
        BLOCK = 64

        def build_slope_tensor(n_heads):

            def p2(n):
                start = 2.0 ** (-2.0 ** (-(math.log2(n) - 3)))
                return [start * start ** i for i in range(n)]
            if math.log2(n_heads).is_integer():
                s = p2(n_heads)
            else:
                closest = 2 ** math.floor(math.log2(n_heads))
                s = p2(closest) + p2(2 * closest)[0::2][:n_heads - closest]
            return jnp.asarray(np.array(s, dtype=np.float32))

        def lightning_attn(q, k, v, slopes, block=BLOCK):
            B, H, N, d = q.shape
            nc = N // block
            i = jnp.arange(block, dtype=q.dtype)
            diff = i[:, None] - i[None, :]
            intra_decay = jnp.where(diff >= 0, jnp.exp(-slopes[:, None, None] * diff), 0.0)
            q_decay = jnp.exp(-slopes[:, None] * i[None, :])
            k_decay = jnp.exp(-slopes[:, None] * (block - i[None, :]))
            blk_decay = jnp.exp(-slopes * block)

            def to_chunks(t):
                return t.reshape(B, H, nc, block, d).transpose(2, 0, 1, 3, 4)
            qc, kc, vc = (to_chunks(q), to_chunks(k), to_chunks(v))

            def body(S, xs):
                qb, kb, vb = xs
                scores = jnp.einsum('bhid,bhjd->bhij', qb, kb) * intra_decay[None]
                o_intra = jnp.einsum('bhij,bhjd->bhid', scores, vb)
                o_inter = jnp.einsum('bhid,bhde->bhie', qb * q_decay[None, :, :, None], S)
                S_new = blk_decay[None, :, None, None] * S + jnp.einsum('bhjd,bhje->bhde', kb * k_decay[None, :, :, None], vb)
                return (S_new, o_intra + o_inter)
            S0 = jnp.zeros((B, H, d, d), dtype=q.dtype)
            _, o = jax.lax.scan(body, S0, (qc, kc, vc))
            return o.transpose(1, 2, 0, 3, 4).reshape(B, H, N, d)
        key = jax.random.key(seed)
        k1, k2, k3 = jax.random.split(key, 3)
        dim, num_heads = (512, 16)
        B, N = (2, 1024)
        x = jax.random.normal(k1, (B, N, dim), dtype=jnp.float32)
        Wqkv = jax.random.normal(k2, (dim, 3 * dim), dtype=jnp.float32) / math.sqrt(dim)
        bqkv = jnp.zeros((3 * dim,), dtype=jnp.float32)
        Wout = jax.random.normal(k3, (dim, dim), dtype=jnp.float32) / math.sqrt(dim)
        bout = jnp.zeros((dim,), dtype=jnp.float32)
        slopes = build_slope_tensor(num_heads)
        return {'x': x, 'Wqkv': Wqkv, 'bqkv': bqkv, 'Wout': Wout, 'bout': bout, 'slopes': slopes}
    _L0_attn_in = _L0_attn_setup()

    def _L0_ffn_setup():
        import jax, jax.numpy as jnp
        import numpy as np
        BLOCK_SIZE = 32
        HIDDEN_SIZE = 512
        MLP_DIM = 4096
        NVFP4_LUT = jnp.array([0.0, 0.5, 1.0, 1.5, 2.0, 3.0, 4.0, 6.0, 0.0, -0.5, -1.0, -1.5, -2.0, -3.0, -4.0, -6.0], dtype=jnp.float32)

        def dequant_nvfp4(W_packed, scales, block=BLOCK_SIZE):
            N = W_packed.shape[0]
            low = W_packed & 15
            high = W_packed >> 4 & 15
            idx = jnp.stack([low, high], axis=-1).reshape(N, -1)
            vals = NVFP4_LUT[idx]
            K = vals.shape[1]
            vals = vals.reshape(N, K // block, block) * scales[:, :, None]
            return vals.reshape(N, K)
        key = jax.random.key(seed)
        ks = jax.random.split(key, 7)
        x = jax.random.normal(ks[0], (4, 32, HIDDEN_SIZE), dtype=jnp.float32)
        gate_W_packed = jax.random.randint(ks[1], (MLP_DIM, HIDDEN_SIZE // 2), 0, 64, dtype=jnp.int32)
        gate_scales = jax.random.uniform(ks[2], (MLP_DIM, HIDDEN_SIZE // BLOCK_SIZE), dtype=jnp.float32) * 0.1 + 0.001
        up_W_packed = jax.random.randint(ks[3], (MLP_DIM, HIDDEN_SIZE // 2), 0, 64, dtype=jnp.int32)
        up_scales = jax.random.uniform(ks[4], (MLP_DIM, HIDDEN_SIZE // BLOCK_SIZE), dtype=jnp.float32) * 0.1 + 0.001
        down_W_packed = jax.random.randint(ks[5], (HIDDEN_SIZE, MLP_DIM // 2), 0, 64, dtype=jnp.int32)
        down_scales = jax.random.uniform(ks[6], (HIDDEN_SIZE, MLP_DIM // BLOCK_SIZE), dtype=jnp.float32) * 0.1 + 0.001
        return {'x': x, 'gate_W_packed': gate_W_packed, 'gate_scales': gate_scales, 'up_W_packed': up_W_packed, 'up_scales': up_scales, 'down_W_packed': down_W_packed, 'down_scales': down_scales}
    _L0_ffn_in = _L0_ffn_setup()
    _L0_c = _w((lambda *s: np.random.randn(*s).astype(np.float32) * 0.05)(1, 512))
    _L0_wmod = _w((lambda *s: np.random.randn(*s).astype(np.float32) * 0.05)(512, 6 * 512) * 512 ** (-0.5))
    _d = {'L0_attn_x': _L0_attn_in['x'], 'L0_attn_Wqkv': _L0_attn_in['Wqkv'], 'L0_attn_bqkv': _L0_attn_in['bqkv'], 'L0_attn_Wout': _L0_attn_in['Wout'], 'L0_attn_bout': _L0_attn_in['bout'], 'L0_attn_slopes': _L0_attn_in['slopes'], 'L0_ffn_gate_W_packed': _L0_ffn_in['gate_W_packed'], 'L0_ffn_gate_scales': _L0_ffn_in['gate_scales'], 'L0_ffn_up_W_packed': _L0_ffn_in['up_W_packed'], 'L0_ffn_up_scales': _L0_ffn_in['up_scales'], 'L0_ffn_down_W_packed': _L0_ffn_in['down_W_packed'], 'L0_ffn_down_scales': _L0_ffn_in['down_scales'], 'L0_c': _L0_c, 'L0_wmod': _L0_wmod}
    _x0 = _d['L0_attn_x']
    _d['L0_attn_x'] = jax.random.normal(jax.random.fold_in(jax.random.key(seed), 1), (1, 2048, 512), dtype=_x0.dtype)
    del _x0
    return _d

def reference(L0_attn_x, L0_attn_Wqkv, L0_attn_bqkv, L0_attn_Wout, L0_attn_bout, L0_attn_slopes, L0_ffn_gate_W_packed, L0_ffn_gate_scales, L0_ffn_up_W_packed, L0_ffn_up_scales, L0_ffn_down_W_packed, L0_ffn_down_scales, L0_c, L0_wmod):

    def _L0_attn_ref(x, Wqkv, bqkv, Wout, bout, slopes):
        import math
        import jax, jax.numpy as jnp
        import numpy as np
        BLOCK = 64

        def build_slope_tensor(n_heads):

            def p2(n):
                start = 2.0 ** (-2.0 ** (-(math.log2(n) - 3)))
                return [start * start ** i for i in range(n)]
            if math.log2(n_heads).is_integer():
                s = p2(n_heads)
            else:
                closest = 2 ** math.floor(math.log2(n_heads))
                s = p2(closest) + p2(2 * closest)[0::2][:n_heads - closest]
            return jnp.asarray(np.array(s, dtype=np.float32))

        def lightning_attn(q, k, v, slopes, block=BLOCK):
            B, H, N, d = q.shape
            nc = N // block
            i = jnp.arange(block, dtype=q.dtype)
            diff = i[:, None] - i[None, :]
            intra_decay = jnp.where(diff >= 0, jnp.exp(-slopes[:, None, None] * diff), 0.0)
            q_decay = jnp.exp(-slopes[:, None] * i[None, :])
            k_decay = jnp.exp(-slopes[:, None] * (block - i[None, :]))
            blk_decay = jnp.exp(-slopes * block)

            def to_chunks(t):
                return t.reshape(B, H, nc, block, d).transpose(2, 0, 1, 3, 4)
            qc, kc, vc = (to_chunks(q), to_chunks(k), to_chunks(v))

            def body(S, xs):
                qb, kb, vb = xs
                scores = jnp.einsum('bhid,bhjd->bhij', qb, kb) * intra_decay[None]
                o_intra = jnp.einsum('bhij,bhjd->bhid', scores, vb)
                o_inter = jnp.einsum('bhid,bhde->bhie', qb * q_decay[None, :, :, None], S)
                S_new = blk_decay[None, :, None, None] * S + jnp.einsum('bhjd,bhje->bhde', kb * k_decay[None, :, :, None], vb)
                return (S_new, o_intra + o_inter)
            S0 = jnp.zeros((B, H, d, d), dtype=q.dtype)
            _, o = jax.lax.scan(body, S0, (qc, kc, vc))
            return o.transpose(1, 2, 0, 3, 4).reshape(B, H, N, d)
        B, N, C = x.shape
        H = slopes.shape[0]
        hd = C // H
        qkv = (x @ Wqkv + bqkv).reshape(B, N, 3, H, hd)
        qkv = qkv.transpose(2, 0, 3, 1, 4)
        q, k, v = (qkv[0], qkv[1], qkv[2])
        attn = lightning_attn(q, k, v, slopes)
        out = attn.transpose(0, 2, 1, 3).reshape(B, N, C)
        return out @ Wout + bout

    def _L0_ffn_ref(x, gate_W_packed, gate_scales, up_W_packed, up_scales, down_W_packed, down_scales):
        import jax, jax.numpy as jnp
        import numpy as np
        BLOCK_SIZE = 32
        HIDDEN_SIZE = 512
        MLP_DIM = 4096
        NVFP4_LUT = jnp.array([0.0, 0.5, 1.0, 1.5, 2.0, 3.0, 4.0, 6.0, 0.0, -0.5, -1.0, -1.5, -2.0, -3.0, -4.0, -6.0], dtype=jnp.float32)

        def dequant_nvfp4(W_packed, scales, block=BLOCK_SIZE):
            N = W_packed.shape[0]
            low = W_packed & 15
            high = W_packed >> 4 & 15
            idx = jnp.stack([low, high], axis=-1).reshape(N, -1)
            vals = NVFP4_LUT[idx]
            K = vals.shape[1]
            vals = vals.reshape(N, K // block, block) * scales[:, :, None]
            return vals.reshape(N, K)
        B, S, H = x.shape
        xt = x.reshape(B * S, H)
        Wg = dequant_nvfp4(gate_W_packed, gate_scales)
        Wu = dequant_nvfp4(up_W_packed, up_scales)
        Wd = dequant_nvfp4(down_W_packed, down_scales)
        gate = jnp.einsum('th,nh->tn', xt, Wg)
        up = jnp.einsum('th,nh->tn', xt, Wu)
        gelu = jnp.tanh(0.7978845608028654 * (gate + 0.044715 * gate ** 3)) * gate * 0.5 + gate * 0.5
        inter = gelu * up
        out = jnp.einsum('tn,hn->th', inter, Wd)
        return out.reshape(B, S, H)
    x = L0_attn_x
    mod = (_silu(L0_c) @ L0_wmod).reshape(L0_c.shape[0], 6, 1, -1)
    sa, ca, ga, sb, cb, gb = (mod[:, 0], mod[:, 1], mod[:, 2], mod[:, 3], mod[:, 4], mod[:, 5])
    ga = (2 * (ga >= 0) - 1) * jnp.maximum(jnp.abs(ga), 0.25)
    gb = (2 * (gb >= 0) - 1) * jnp.maximum(jnp.abs(gb), 0.25)
    h = _layernorm(x, axis=-1) * (1 + ca) + sa
    x = x + ga * _L0_attn_ref(h, L0_attn_Wqkv, L0_attn_bqkv, L0_attn_Wout, L0_attn_bout, L0_attn_slopes)
    h = _layernorm(x, axis=-1) * (1 + cb) + sb
    x = x + gb * _L0_ffn_ref(h, L0_ffn_gate_W_packed, L0_ffn_gate_scales, L0_ffn_up_W_packed, L0_ffn_up_scales, L0_ffn_down_W_packed, L0_ffn_down_scales)
    return x

_drawn_inputs = setup_inputs


def setup_inputs(seed=0):
    import zlib

    import numpy as np

    out = dict(_drawn_inputs(seed))
    spreads = {'L0_attn_bqkv': (0.0, 0.1), 'L0_attn_bout': (0.0, 0.8)}
    factors = {}
    for name, (base, spread) in spreads.items():
        noise = np.random.default_rng([zlib.crc32(name.encode()), seed]).standard_normal(out[name].shape)
        drawn = base * np.exp(spread * noise) if base else spread * noise
        out[name] = jnp.asarray(drawn.astype(out[name].dtype))
    for name, factor in factors.items():
        out[name] = (out[name] * factor).astype(out[name].dtype)
    return out
```

```python
from contextlib import ExitStack

import concourse.bass as bass
from concourse import mybir

F32 = mybir.dt.float32
F16 = mybir.dt.float16
I32 = mybir.dt.int32
ALU = mybir.AluOpType
ACT = mybir.ActivationFunctionType

P = 128
N = 2048
D = 512
KT = D // P
H = 16
HD = D // H
R = P // HD
C = P
NCH = N // C
GC = 4
G = NCH // GC
GT = GC * C
F = 4096
FC = 512
NF = F // FC
FT = FC // P
NT = N // GT
STEPS = NT * FT
UNITS = 12
EPS = 1e-5

W_SCALE = 2.0 ** 8
ATT_SCALE = 2.0 ** -4
MLP_SCALE = 2.0 ** -3
CODE_SCALE = 2.0 ** 14
CODE_MASK = 0x8E000000 - (1 << 32)
GELU_A = 0.7978845608028654
GELU_B = 0.044715


def adaln_block_kernel(nc, x, wmod, cond, wqkv, bqkv, bqk_cols, wout, bout, slopes, slopes_rg, codes, scales, out):
    with ExitStack() as ctx:
        def sb(name, shape, dt=F32):
            return ctx.enter_context(nc.sbuf_tensor(name, shape, dt))

        def sem(name):
            return ctx.enter_context(nc.semaphore(name))

        xs = sb("xs", [P, NCH * D])
        h2 = sb("h2", [P, 2 * KT * N], F16)
        h2hi = h2[:, 0:KT * N].rearrange("p (k t) -> p k t", k=KT)
        h2lo = h2[:, KT * N:2 * KT * N].rearrange("p (k t) -> p k t", k=KT)
        h2_f32 = h2[:, :].bitcast(F32)
        wq_in = [h2_f32[:, j * 2048:(j + 1) * 2048].rearrange("p (k n) -> p k n", k=KT) for j in range(3)]
        wo_in = h2_f32[:, 6144:8192].rearrange("p (k n) -> p k n", k=KT)

        wa = sb("wa", [P, 2 * KT * 3 * D], F16)
        wqkv_hl = wa[:, :].rearrange("p (s k n) -> p s k n", s=2, k=KT)
        qkv = sb("qkv", [P, 3 * KT * GT])
        qT = qkv[:, 0:2048].rearrange("p (g t) -> p g t", g=KT)
        kT = qkv[:, 2048:4096].rearrange("p (g t) -> p g t", g=KT)
        vv = qkv[:, 4096:6144].rearrange("p (c n) -> p c n", c=GC)
        wb = qkv[:, :].bitcast(F16)
        ffw = [w.rearrange("p (s t b m n) -> p s t b m n", s=2, t=2, b=2, m=3) for w in (wa[:, :], wb)]

        wo = sb("wo", [P, 2 * KT * D], F16)
        wo_hl = wo[:, :].rearrange("p (s k n) -> p s k n", s=2, k=KT)
        h1 = sb("h1", [P, 2 * KT * GT], F16)
        h1_hl = h1[:, :].rearrange("p (s k t) -> p s k t", s=2, k=KT)

        stage = sb("stage", [P, 4608])
        wm_in = [stage[:, j * 2048:(j + 1) * 2048].rearrange("p (k n) -> p k n", k=KT) for j in range(2)]
        pk = stage[:, 0:3072].bitcast(I32).rearrange("p (t m n) -> p t m n", t=2, m=3)
        scl = [stage[:, 3072:4608].rearrange("p (m n) -> p m n", m=3),
               h1[:, 0:3072].bitcast(F32).rearrange("p (m n) -> p m n", m=3)]

        mask = sb("mask", [P, R * KT * C])
        mask_r = mask[:, :].rearrange("p (r n) -> p r n", r=R)
        pr = sb("pr", [P, R * KT * C])
        pr_r = pr[:, :].rearrange("p (r n) -> p r n", r=R)
        pr_rg = pr[:, :].rearrange("p (r g i) -> p r g i", r=R, g=KT)
        colsum = [pr[:, j * D:(j + 1) * D] for j in range(2)]
        gt = [pr[:, 2 * D:3 * D], pr[:, 3 * D:4 * D]]
        T = [mask[:, j * D:(j + 1) * D] for j in range(2)]
        zhl = pr[:, 0:2 * D].bitcast(F16).rearrange("p (b s n) -> p b s n", b=2, s=2)

        qdec = sb("qdec", [P, KT * C])
        kdec = sb("kdec", [P, H])
        sdec = sb("sdec", [P, D])
        bmask = sb("bmask", [P, D])
        kd = sb("kd", [P, D])
        qd = sb("qd", [P, KT * C])
        S = sb("S", [P, 2, D])
        s_dec = sb("s_dec", [P, D])
        s_new = sb("s_new", [P, D])
        att = sb("att", [P, D])
        att_hl = sb("att_hl", [P, 2, D], F16)
        ht = [sb("ht1", [P, D]), sb("ht2", [P, D])]
        xint = sb("xint", [P, D], I32)
        sca = sb("sca", [P, 2, D])
        wf = sca
        sa_bc, ca_bc = sca[:, 0, :], sca[:, 1, :]
        sb_bc, cb_bc, gb_bc = (sb(n, [P, D]) for n in ("sb_bc", "cb_bc", "gb_bc"))
        ga_bc = att
        bga = sb("bga", [P, D])
        bv_bc = sb("bv_bc", [P, D])
        ident = sb("ident", [P, P])
        ones = sb("ones", [P, P])
        dif = s_new[:, 0:P].bitcast(I32)
        difc = gt[0][:, 0:P]
        ge = gt[0][:, P:2 * P]
        idx = gt[0][:, 2 * P:3 * P]
        small = sb("small", [P, 96])
        cT, ce, c1, sil = (small[:, 4 * j:4 * j + 4] for j in range(4))
        spart = small[:, 16:20]
        nsp = small[:, 20:24]
        bdec = small[:, 24:28]
        bqk = small[:, 28:36]
        nsl = small[:, 36:52]
        cj = small[:, 52:53]
        epow = small[:, 53:54]
        stat = [small[:, 54:60], small[:, 60:66]]
        mv = [small[:, 66:68], small[:, 68:70]]
        ve = [small[:, 70:71], small[:, 71:72]]
        rs = [small[:, 72:73], small[:, 73:74]]
        slp = small[:, 76:92]
        tick = small[:, 92:93]
        epsc = small[:, 93:94]
        ints = sb("ints", [P, 1], I32)
        idxi = xint[:, 0:P]

        B = [ctx.enter_context(nc.psum_tensor(f"bank{b}", [P, 512], F32)) for b in range(8)]

        in_small, in_wmod0, in_wmod1, in_x0, in_x, in_wout = (
            sem(n) for n in ("in_small", "in_wmod0", "in_wmod1", "in_x0", "in_x", "in_wout"))
        in_cond = sem("in_cond")
        in_wmod = [in_wmod0, in_wmod1]
        in_wq = [sem(f"in_wq{j}") for j in range(3)]
        in_half = [sem("in_half0"), sem("in_half1")]
        out_done = sem("out_done")
        iota_done, const_done, exp_done, mask_done, sdec_done = (
            sem(n) for n in ("iota_done", "const_done", "exp_done", "mask_done", "sdec_done"))
        silu_exp, silu_done, colsum_done, mod_mm, mod_row, gates_done = (
            sem(n) for n in ("silu_exp", "silu_done", "colsum_done", "mod_mm", "mod_row", "gates_done"))
        wq_hi, wq_lo, wo_f, wo_hi, wo_lo = (sem(n) for n in ("wq_hi", "wq_lo", "wo_f", "wo_hi", "wo_lo"))
        dve_chain, pool_chain = sem("dve_chain"), sem("pool_chain")
        stats_done = [sem("stats1_done"), sem("stats2_done")]
        rstd_done = [sem("rstd1_done"), sem("rstd2_done")]
        norm_done = [sem("norm1_done"), sem("norm2_done")]
        ht_done = [sem("ht1_done"), sem("ht2_done")]
        lt_done = [sem("lt1_done"), sem("lt2_done")]
        hhi_done = [sem("h1hi_done"), sem("h2hi_done")]
        hlo_done = [sem("h1lo_done"), sem("h2lo_done")]
        xb_done, x1_done = sem("xb_done"), sem("x1_done")
        qk_mm, qk_done, v_mm, v_done = (sem(n) for n in ("qk_mm", "qk_done", "v_mm", "v_done"))
        kt_mm, kd_done, sc_mm, pr_done = (sem(n) for n in ("kt_mm", "kd_done", "sc_mm", "pr_done"))
        st_mm, snew_done, sdecay_done, S_done, qd_done = (
            sem(n) for n in ("st_mm", "snew_done", "sdecay_done", "S_done", "qd_done"))
        av_mm, att_done, at_mm, ahi_done, alo_done, wo_mm = (
            sem(n) for n in ("av_mm", "att_done", "at_mm", "ahi_done", "alo_done", "wo_mm"))
        wf_done, whi_done, wlo_done = (sem(n) for n in ("wf_done", "whi_done", "wlo_done"))
        gate_mm, up_mm, dn_mm = (sem(n) for n in ("gate_mm", "up_mm", "dn_mm"))
        sq_done, u_done, th_done, w_done, z_done, zhi_done, zlo_done, acc_done = (
            sem(n) for n in ("sq_done", "u_done", "th_done", "w_done", "z_done", "zhi_done", "zlo_done", "acc_done"))

        block = ctx.enter_context(nc.Block())

        def wait(eng, s_, v_):
            if not (isinstance(v_, int) and v_ <= 0):
                eng.wait_ge(s_, v_)

        def xrow(n):
            return xs[:, bass.ds(n * D, D)]

        MODS = ["sa", "ca", "ga", "sb", "cb", "gb"]
        SETUP = [0, 1, 2, 3, 4, 5]

        def half_of(c):
            return c // 2, c % 2

        @block.sync
        def _(sp):
            sp.dma_start(cT, cond).then_inc(in_cond, 16)
            wm = wmod.rearrange("(k p) (s n) -> p k s n", p=P, s=6)

            def load_wmod(j):
                if j >= 2:
                    sp.wait_ge(colsum_done, j - 1)
                sp.dma_start(wm_in[j % 2], wm[:, :, SETUP[j], :]).then_inc(in_wmod[j % 2], 16)

            xv = x.rearrange("(g c p) n -> g p c n", p=P, c=GC)
            load_wmod(0)
            sp.dma_start(xs[:, 0:GC * D].rearrange("p (c n) -> p c n", c=GC), xv[0]).then_inc(in_x0, 16)
            load_wmod(1)
            for r in range(R):
                sp.dma_start(spart[HD * r:HD * r + HD, :],
                             slopes_rg[r:r + 1, :].to_broadcast([HD, KT])).then_inc(in_small, 16)
            row = slopes.rearrange("(a n) -> a n", a=1)
            sp.dma_start(slp, row.to_broadcast([P, H])).then_inc(in_small, 16)
            sp.dma_start(bqk, bqk_cols).then_inc(in_small, 16)
            brow = bqkv.rearrange("(a n) -> a n", a=1)
            sp.dma_start(bv_bc[:, :], brow[:, 2 * D:3 * D].to_broadcast([P, D])).then_inc(in_small, 16)
            sp.dma_start(bga[:, :], bout.rearrange("(a n) -> a n", a=1).to_broadcast([P, D])).then_inc(in_small, 16)
            wqv = wqkv.rearrange("(k p) (j n) -> j p k n", p=P, j=3)
            for j in range(3):
                sp.dma_start(wq_in[j], wqv[j]).then_inc(in_wq[j], 16)
            for j in range(2, 6):
                load_wmod(j)
            sp.dma_start(wo_in, wout.rearrange("(k p) n -> p k n", p=P)).then_inc(in_wout, 16)
            for g in range(1, G):
                sp.dma_start(xs[:, g * GC * D:(g + 1) * GC * D].rearrange("p (c n) -> p c n", c=GC),
                             xv[g]).then_inc(in_x, 16)

            def load_half(c, t):
                sp.dma_start(pk[:, t, :, :], codes[bass.ds(c, 1), t].rearrange("a p m n -> (a p) m n")).then_inc(in_half[t], 16)
                src = scales[bass.ds(c, 1), t].rearrange("a b m n -> (a b) (m n)").unsqueeze(1)
                sp.dma_start(scl[t].rearrange("p m n -> p (m n)"),
                             src.to_broadcast([8, 16, 3 * D])).then_inc(in_half[t], 16)

            sp.wait_ge(colsum_done, 6)
            load_half(0, 0)
            sp.wait_ge(v_mm, NCH)
            load_half(0, 1)
            with sp.Fori(1, NF) as c:
                for t in range(2):
                    sp.wait_ge(wf_done, c * UNITS - UNITS + 6 * (t + 1))
                    load_half(c, t)
            ov = out.rearrange("(n p) d -> n p d", p=P)
            for n in range(NCH):
                sp.wait_ge(acc_done, NCH * (NF - 1) + n + 1)
                sp.dma_start(ov[n], xs[:, n * D:(n + 1) * D]).then_inc(out_done, 16)
            sp.wait_ge(out_done, 16 * NCH)

        @block.gpsimd
        def _(pool):
            nc.gpsimd.iota(dif, pattern=[[1, P]], base=0, channel_multiplier=-1).then_inc(iota_done, 1)
            nc.gpsimd.iota(idxi, pattern=[[1, P]], base=0, channel_multiplier=0).then_inc(iota_done, 1)
            nc.gpsimd.iota(ints[:, :], pattern=[[1, 1]], base=C, channel_multiplier=-1).then_inc(iota_done, 1)
            nc.gpsimd.memset(epow, -0.5)
            nc.gpsimd.memset(epsc, EPS).then_inc(pool_chain, 1)
            chain = [1]

            def rstd(ln, n, base):
                pool.wait_ge(stats_done[ln], n + 1)
                nc.gpsimd.tensor_tensor(ve[ln], mv[ln][:, 1:2], epsc, ALU.add).then_inc(pool_chain, 1)
                pool.wait_ge(pool_chain, base + 1)
                nc.gpsimd.tensor_tensor(rs[ln], ve[ln], epow, ALU.pow).then_inc(rstd_done[ln], 1)

            def modulate(ln, n, base):
                pool.wait_ge(norm_done[ln], n + 1)
                nc.gpsimd.tensor_tensor(ht[ln][:, :], ht[ln][:, :], (ca_bc, cb_bc[:, :])[ln], ALU.mult).then_inc(pool_chain, 1)
                pool.wait_ge(pool_chain, base + 1)
                nc.gpsimd.tensor_tensor(ht[ln][:, :], ht[ln][:, :], (sa_bc, sb_bc[:, :])[ln], ALU.add).then_inc(ht_done[ln], 1)

            def layer_norm(ln, n, base):
                rstd(ln, n, base)
                modulate(ln, n, base + 1)

            def add_bias(m):
                nc.gpsimd.tensor_tensor(xrow(m), xrow(m), bga[:, :], ALU.add).then_inc(xb_done, 1)

            def slot(n, c, base, lo_ln1, lo_ln2):
                if c == 0:
                    pool.wait_ge(qk_done, (n + GC) * 2)
                wait(pool, av_mm, n)
                nc.gpsimd.tensor_tensor(qd[:, :].rearrange("p (g i) -> p g i", g=KT), qT[:, :, c * C:(c + 1) * C],
                                        qdec[:, :].rearrange("p (g i) -> p g i", g=KT), ALU.mult).then_inc(qd_done, 1)
                pool.wait_ge(S_done, n + 1)
                nc.gpsimd.tensor_tensor(s_dec[:, :], S[:, c % 2, :], sdec[:, :], ALU.mult).then_inc(sdecay_done, 1)
                k = 0
                if lo_ln1:
                    layer_norm(0, n + GC, base + k)
                    add_bias(n + GC)
                    k += 2
                if lo_ln2:
                    layer_norm(1, n - 1, base + k)
                    k += 2
                return k

            pool.wait_ge(pool_chain, 1)
            pool.wait_ge(mod_row, 2)
            for m in range(GC):
                layer_norm(0, m, chain[0])
                chain[0] += 2
            pool.wait_ge(gates_done, 2)
            for m in range(GC):
                add_bias(m)
            pool.wait_ge(sdec_done, 1)

            def group(g, base, first=False, last=False):
                k = 0
                if not first:
                    layer_norm(1, g * GC - 1, base)
                    k += 2
                for c in range(GC):
                    k += slot(g * GC + c, c, base + k, not last, c > 0)
                return k

            pool.wait_ge(mod_row, 6)
            chain[0] += group(0, chain[0], first=True)
            per = 2 + 2 * GC + 2 * (GC - 1)
            base = chain[0]
            with pool.Fori(1, G - 1) as g:
                assert group(g, (g - 1) * per + base) == per
            group(G - 1, base + (G - 2) * per, last=True)
            layer_norm(1, NCH - 1, base + (G - 2) * per + 2 + 2 * (GC - 1))

        @block.scalar
        def _(act):
            act.wait_ge(in_cond, 16)
            nc.scalar.activation(ce, cT, ACT.Exp, scale=-1.0).then_inc(silu_exp, 1)
            dst = {"sa": sa_bc, "ca": ca_bc, "ga": ga_bc[:, :], "sb": sb_bc[:, :], "cb": cb_bc[:, :], "gb": gb_bc[:, :]}

            def mod_rows(j):
                name = MODS[SETUP[j]]
                act.wait_ge(mod_mm, j + 1)
                nc.scalar.activation(dst[name], B[6 + j % 2][:, :], ACT.Identity,
                                     bias=ones[:, 0:1] if name in ("ca", "cb") else 0.0).then_inc(mod_row, 1)

            def split_hi(ln, m, col):
                act.wait_ge(lt_done[ln], m + 1)
                dstT = h1_hl[:, 0, :, col:col + C] if ln == 0 else h2hi[:, :, bass.ds(col, C)]
                nc.scalar.copy(dstT, B[(5, 7)[ln]][:, :].rearrange("p (k t) -> p k t", k=KT)).then_inc(hhi_done[ln], 1)

            mod_rows(0)
            mod_rows(1)
            for j in range(3):
                act.wait_ge(in_wq[j], 16)
                for k in range(KT):
                    nc.scalar.activation(wqkv_hl[:, 0, k, j * D:(j + 1) * D], wq_in[j][:, k, :], ACT.Copy,
                                         scale=W_SCALE).then_inc(wq_hi, 1)
                if j == 0:
                    split_hi(0, 0, 0)
                    split_hi(0, 1, C)
            split_hi(0, 2, 2 * C)
            split_hi(0, 3, 3 * C)
            act.wait_ge(const_done, 1)
            nc.scalar.activation(bdec, nsp, ACT.Exp, scale=float(C)).then_inc(exp_done, 1)
            nc.scalar.activation(kdec[:, :], nsl, ACT.Exp, scale=cj).then_inc(exp_done, 1)
            for g in range(KT):
                nc.scalar.activation(qdec[:, g * C:(g + 1) * C], idx, ACT.Exp, scale=nsp[:, g:g + 1]).then_inc(exp_done, 1)
            for r in range(R):
                for g in range(KT):
                    h = R * g + r
                    nc.scalar.activation(mask_r[:, r, g * C:(g + 1) * C], difc, ACT.Exp,
                                         scale=nsl[:, h:h + 1]).then_inc(exp_done, 1)

            def att_hi(n):
                act.wait_ge(at_mm, n + 1)
                nc.scalar.activation(att_hl[:, 0, :], B[7][:, :], ACT.Copy, scale=ATT_SCALE).then_inc(ahi_done, 1)

            def qk_out(g, i):
                act.wait_ge(qk_mm, g * 8 + i + 1)
                dstT = (qT, kT)[i % 2][:, i // 2, :]
                col = (i % 2) * KT + i // 2
                nc.scalar.activation(dstT, B[i % 4][:, :], ACT.Identity, bias=bqk[:, col:col + 1],
                                     scale=1.0 / W_SCALE).then_inc(qk_done, 1)

            def group(g, first=False, last=False):
                for i in range(8):
                    qk_out(g, i)
                    if first and i < 4:
                        mod_rows(2 + i)
                    if not first:
                        if i == 0:
                            att_hi(g * GC - 1)
                        if i == 1:
                            split_hi(1, g * GC - 2, (g * GC - 2) * C)
                        if i == 6:
                            split_hi(1, g * GC - 1, (g * GC - 1) * C)
                if first:
                    for k in range(KT):
                        act.wait_ge(wo_f, k + 1)
                        nc.scalar.copy(wo_hl[:, 0, k, :], wo_in[:, k, :]).then_inc(wo_hi, 1)
                for c in range(GC):
                    n = g * GC + c
                    if c > 0:
                        att_hi(n - 1)
                    if last:
                        t, b = half_of(c)
                        for m in range(3):
                            act.wait_ge(wf_done, 3 * c + m + 1)
                            act.wait_ge(v_mm, NCH)
                            nc.scalar.copy(ffw[0][:, 0, t, b, m, :], wf[:, (3 * c + m) % 2, :]).then_inc(whi_done, 1)
                    act.wait_ge(av_mm, n + 1)
                    nc.scalar.copy(att[:, :], B[6][:, :]).then_inc(att_done, 1)
                    if not last:
                        split_hi(0, n + GC, c * C)
                    if c > 1:
                        split_hi(1, n - 2, (n - 2) * C)

            group(0, first=True)
            with act.Fori(1, G - 1) as g:
                group(g)
            group(G - 1, last=True)
            att_hi(NCH - 1)
            split_hi(1, NCH - 2, (NCH - 2) * C)
            split_hi(1, NCH - 1, (NCH - 1) * C)

            def chunk(c, par, first=False, last=False):
                for t in range(NT):
                    for ft in range(FT):
                        s = c * STEPS + (t * FT + ft)
                        b = ft % 2
                        act.wait_ge(gate_mm, s + 1)
                        if not (first and t == 0 and ft < 2):
                            act.wait_ge(zlo_done, s - 1)
                        nc.scalar.activation(T[b], B[b][:, :], ACT.Square, scale=1.0 / W_SCALE).then_inc(sq_done, 1)
                        act.wait_ge(u_done, s + 1)
                        nc.scalar.activation(T[b], T[b], ACT.Tanh, scale=GELU_A * GELU_B / W_SCALE).then_inc(th_done, 1)
                        if ft > 0 and not last:
                            th, nib, m = t // 2, t % 2, ft - 1
                            i = 3 * t + m
                            act.wait_ge(wf_done, c * UNITS + (UNITS + i + 1))
                            wait(act, dn_mm, c * (STEPS * GC))
                            nc.scalar.copy(ffw[1 - par][:, 0, th, nib, m, :], wf[:, i % 2, :]).then_inc(whi_done, 1)
                        act.wait_ge(z_done, s + 1)
                        if not (first and t == 0 and ft < 2):
                            act.wait_ge(dn_mm, c * (STEPS * GC) + GC * (t * FT + ft - 1))
                        nc.scalar.copy(zhl[:, b, 0, :], T[b]).then_inc(zhi_done, 1)

            chunk(0, 0, first=True)
            with act.Fori(0, (NF - 2) // 2) as cp:
                chunk(cp * 2 + 1, 1)
                chunk(cp * 2 + 2, 0)
            chunk(NF - 1, 1, last=True)

        @block.vector
        def _(dve):
            links = [0]

            def link(ins, base, k):
                ins.then_inc(dve_chain, 1)
                dve.wait_ge(dve_chain, base + k)

            def link0(ins):
                links[0] += 1
                link(ins, links[0], 0)

            V = nc.vector
            V.memset(ones[:, :], 1.0)
            link0(V.memset(bmask[:, :], 0.0))
            V.memset(S[:, 0, :], 0.0).then_inc(S_done, 1)
            for r in range(R):
                V.memset(bmask[HD * r:HD * r + HD, :].rearrange("p (g e) -> p g e", g=KT)[:, :, HD * r:HD * r + HD], 1.0)
            dve.wait_ge(iota_done, 3)
            V.tensor_scalar(ident[:, :], dif, 0.0, None, ALU.is_equal)
            V.tensor_scalar(difc, dif, 0.0, None, ALU.max)
            V.tensor_scalar(ge, dif, 0.0, None, ALU.is_ge)
            V.tensor_copy(idx, idxi)
            V.tensor_copy(cj, ints[:, :])
            dve.wait_ge(in_cond, 16)
            dve.wait_ge(silu_exp, 1)
            link0(V.tensor_scalar(c1, ce, 1.0, None, ALU.add))
            link0(V.reciprocal(ce, c1))
            link0(V.tensor_tensor(sil, cT, ce, ALU.mult))

            def mod_sum(j):
                dve.wait_ge(in_wmod[j % 2], 16 * (j // 2 + 1))
                if j >= 2:
                    dve.wait_ge(mod_mm, j - 1)
                w, t = wm_in[j % 2], colsum[j % 2]
                link0(V.tensor_scalar(t, w[:, 0, :], sil[:, 0:1], None, ALU.mult))
                for k in range(1, KT):
                    ins = V.scalar_tensor_tensor(t, w[:, k, :], sil[:, k:k + 1], t, ALU.mult, ALU.add)
                    if k < KT - 1:
                        link0(ins)
                ins.then_inc(colsum_done, 1)

            mod_sum(0)
            mod_sum(1)
            dve.wait_ge(in_small, 16 * 8)
            V.tensor_scalar(nsp, spart, -1.0, None, ALU.mult)
            V.tensor_scalar(nsl, slp, -1.0, None, ALU.mult).then_inc(const_done, 1)

            def stats(ln, n, base, k):
                V.bn_stats(stat[ln], xrow(n)).then_inc(dve_chain, 1)
                dve.wait_ge(dve_chain, base + k)
                V.memset(tick, 0.0)
                V.bn_aggr(mv[ln], stat[ln]).then_inc(stats_done[ln], 1)

            def normalise(ln, n):
                dve.wait_ge(rstd_done[ln], n + 1)
                wait(dve, lt_done[ln], n)
                V.tensor_scalar(ht[ln][:, :], xrow(n), mv[ln][:, 0:1], rs[ln], ALU.subtract,
                                ALU.mult).then_inc(norm_done[ln], 1)

            def split_lo(ln, m, col):
                dve.wait_ge(hhi_done[ln], m + 1)
                dstT = (h1_hl[:, :, :, col:col + C] if ln == 0 else None)
                hi = dstT[:, 0] if ln == 0 else h2hi[:, :, bass.ds(col, C)]
                lo = dstT[:, 1] if ln == 0 else h2lo[:, :, bass.ds(col, C)]
                V.tensor_tensor(lo, B[(5, 7)[ln]][:, :].rearrange("p (k t) -> p k t", k=KT), hi,
                                ALU.subtract).then_inc(hlo_done[ln], 1)

            def wq_split(j):
                for k in range(KT):
                    dve.wait_ge(wq_hi, j * KT + k + 1)
                    V.scalar_tensor_tensor(wqkv_hl[:, 1, k, j * D:(j + 1) * D], wq_in[j][:, k, :], W_SCALE,
                                           wqkv_hl[:, 0, k, j * D:(j + 1) * D], ALU.mult,
                                           ALU.subtract).then_inc(wq_lo, 1)

            dve.wait_ge(in_x0, 16)
            for m in range(GC):
                links[0] += 1
                stats(0, m, links[0], 0)
                normalise(0, m)
                if m > 0:
                    split_lo(0, m - 1, (m - 1) * C)
                wq_split(m) if m < 3 else None
            split_lo(0, GC - 1, (GC - 1) * C)
            dve.wait_ge(exp_done, 6 + R * KT)
            for r in range(R):
                m3 = mask_r[:, r, :].rearrange("p (g i) -> p g i", g=KT)
                V.tensor_tensor(m3, m3, ge.unsqueeze(1).to_broadcast([P, KT, C]), ALU.mult).then_inc(mask_done, 1)
            for g in range(KT):
                ins = V.tensor_scalar(sdec[:, g * C:(g + 1) * C], bmask[:, g * C:(g + 1) * C], bdec[:, g:g + 1],
                                      None, ALU.mult)
            ins.then_inc(sdec_done, 1)
            for j in range(2, 6):
                mod_sum(j)

            def guard(g_bc):
                V.tensor_scalar(gt[0], g_bc[:, :], 0.0, 2.0, ALU.is_ge, ALU.mult)
                link0(V.scalar_tensor_tensor(gt[1], g_bc[:, :], -1.0, g_bc[:, :], ALU.mult, ALU.max))
                link0(V.tensor_scalar(gt[1], gt[1], 0.25, None, ALU.max))
                return V.scalar_tensor_tensor(g_bc[:, :], gt[0], -1.0, gt[1], ALU.add, ALU.mult)

            dve.wait_ge(mask_done, R)
            dve.wait_ge(mod_row, 3)
            guard(ga_bc).then_inc(gates_done, 1)
            dve.wait_ge(gates_done, 1)
            V.tensor_tensor(bga[:, :], bga[:, :], ga_bc[:, :], ALU.mult).then_inc(gates_done, 1)
            dve.wait_ge(in_wout, 16)
            for k in range(KT):
                V.scalar_tensor_tensor(wo_in[:, k, :], wo_in[:, k, :], W_SCALE, ga_bc[:, :], ALU.mult,
                                       ALU.mult).then_inc(wo_f, 1)
            dve.wait_ge(mod_row, 6)
            guard(gb_bc).then_inc(gates_done, 1)
            dve.wait_ge(gates_done, 3)

            def att_lo(n):
                dve.wait_ge(ahi_done, n + 1)
                V.scalar_tensor_tensor(att_hl[:, 1, :], B[7][:, :], ATT_SCALE, att_hl[:, 0, :], ALU.mult,
                                       ALU.subtract).then_inc(alo_done, 1)

            def residual(n, k0, base):
                dve.wait_ge(wo_mm, n + 1)
                dve.wait_ge(xb_done, n + 1)
                V.scalar_tensor_tensor(xrow(n), B[4][:, :], 1.0 / (W_SCALE * ATT_SCALE), xrow(n), ALU.mult,
                                       ALU.add).then_inc(x1_done, 1)
                dve.wait_ge(x1_done, n + 1)
                V.memset(tick, 0.0)
                stats(1, n, base, k0)

            def v_out(g, c):
                dve.wait_ge(v_mm, g * GC + c + 1)
                V.scalar_tensor_tensor(vv[:, c, :], B[c][:, :], 1.0 / W_SCALE, bv_bc[:, :], ALU.mult,
                                       ALU.add).then_inc(v_done, 1)

            def decode(cpar_unit, th, nib, m, U, first_use, k, base):
                codes_t = pk[:, th, m, :]
                sc_t = scl[th][:, m, :]
                used = 0
                if m == 2 and nib == 0:
                    V.tensor_tensor(sc_t, sc_t, gb_bc[:, :], ALU.mult)
                used += 1
                link(V.tensor_scalar(xint[:, :], codes_t, 28 - 4 * nib, 3, ALU.logical_shift_left,
                                     ALU.arith_shift_right), base, k + used)
                used += 1
                link(V.tensor_scalar(xint[:, :], xint[:, :], CODE_MASK, None, ALU.bitwise_and), base, k + used)
                val = xint[:, :].bitcast(F16).rearrange("p (n two) -> p n two", two=2)[:, :, 1]
                V.scalar_tensor_tensor(wf[:, cpar_unit % 2, :], val, CODE_SCALE * W_SCALE, sc_t, ALU.mult,
                                       ALU.mult).then_inc(wf_done, 1)
                return used

            def weight_lo(cpar_unit, U, dstW):
                dve.wait_ge(whi_done, U + 1)
                V.tensor_tensor(dstW[:, 1], wf[:, cpar_unit % 2, :], dstW[:, 0], ALU.subtract).then_inc(wlo_done, 1)

            def slot(n, c, base, last):
                k = 0
                if not last:
                    k += 1
                    stats(0, n + GC, base, k)
                dve.wait_ge(kt_mm, n + 1)
                V.tensor_tensor(kd[:, :].rearrange("p (h d) -> p h d", h=H), B[4][:, :].rearrange("p (h d) -> p h d", h=H),
                                kdec[:, :].unsqueeze(2).to_broadcast([P, H, HD]), ALU.mult).then_inc(kd_done, 1)
                for r in range(R):
                    dve.wait_ge(sc_mm, R * n + r + 1)
                    V.tensor_tensor(pr_r[:, r, :], B[r][:, :], mask_r[:, r, :], ALU.mult).then_inc(pr_done, 1)
                    if r == 1:
                        if not last:
                            normalise(0, n + GC)
                        if c > 0:
                            att_lo(n - 1)
                dve.wait_ge(st_mm, n + 1)
                V.tensor_tensor(s_new[:, :], B[5][:, :], bmask[:, :], ALU.mult).then_inc(snew_done, 1)
                dve.wait_ge(snew_done, n + 1)
                dve.wait_ge(sdecay_done, n + 1)
                V.tensor_tensor(S[:, (c + 1) % 2, :], s_dec[:, :], s_new[:, :], ALU.add).then_inc(S_done, 1)
                if c > 0:
                    k += 1
                    residual(n - 1, k, base)
                if last:
                    t, b = half_of(c)
                    if c % 2 == 0:
                        dve.wait_ge(in_half[t], 32)
                    for m in range(3):
                        k += decode(3 * c + m, t, b, m, 3 * c + m, None, k, base)
                        weight_lo(3 * c + m, 3 * c + m, ffw[0][:, :, t, b, m, :])
                if not last:
                    split_lo(0, n + GC, c * C)
                if c > 0:
                    normalise(1, n - 1)
                if c > 1:
                    split_lo(1, n - 2, (n - 2) * C)
                return k

            def group(g, base, first=False, last=False):
                k = 0
                if not first:
                    p3 = g * GC - 1
                    att_lo(p3)
                    split_lo(1, p3 - 1, (p3 - 1) * C)
                    k += 1
                    residual(p3, k, base)
                    normalise(1, p3)
                    split_lo(1, p3, p3 * C)
                for c in range(GC):
                    v_out(g, c)
                if first:
                    for kk in range(KT):
                        dve.wait_ge(wo_hi, kk + 1)
                        V.tensor_tensor(wo_hl[:, 1, kk, :], wo_in[:, kk, :], wo_hl[:, 0, kk, :],
                                        ALU.subtract).then_inc(wo_lo, 1)
                    dve.wait_ge(in_x, 16 * (G - 1))
                for c in range(GC):
                    k += slot(g * GC + c, c, base + k, last)
                return k

            links[0] += group(0, links[0], first=True)
            base = links[0]
            per = 1 + GC + (GC - 1)
            with dve.Fori(1, G - 1) as g:
                assert group(g, (g - 1) * per + base) == per
            links[0] = base + (G - 2) * per
            links[0] += group(G - 1, links[0], last=True)
            att_lo(NCH - 1)
            split_lo(1, NCH - 2, (NCH - 2) * C)
            links[0] += 1
            residual(NCH - 1, 0, links[0])
            normalise(1, NCH - 1)
            split_lo(1, NCH - 1, (NCH - 1) * C)

            def accumulate(tile_no, t):
                for q in range(GC):
                    n = t * GC + q
                    dve.wait_ge(dn_mm, tile_no * (FT * GC) + ((FT - 1) * GC + q + 1))
                    V.scalar_tensor_tensor(xs[:, n * D:(n + 1) * D], B[4 + q][:, :], 1.0 / (W_SCALE * MLP_SCALE),
                                           xs[:, n * D:(n + 1) * D], ALU.mult, ALU.add).then_inc(acc_done, 1)

            def chunk(c, par, base, first=False, last=False):
                k = 0
                for t in range(NT):
                    for ft in range(FT):
                        s = c * STEPS + (t * FT + ft)
                        b = ft % 2
                        unit = ft > 0 and not last
                        th, nib, m = t // 2, t % 2, ft - 1
                        i = 3 * t + m
                        dve.wait_ge(sq_done, s + 1)
                        V.scalar_tensor_tensor(T[b], T[b], 1.0 / GELU_B, B[b][:, :], ALU.add, ALU.mult).then_inc(u_done, 1)
                        if unit:
                            if ft == 1 and t % 2 == 0:
                                dve.wait_ge(in_half[th], (c + 2) * 32)
                            k += decode(i, th, nib, m, None, None, k, base)
                        dve.wait_ge(th_done, s + 1)
                        V.scalar_tensor_tensor(T[b], T[b], 1.0, B[b][:, :], ALU.add, ALU.mult).then_inc(w_done, 1)
                        dve.wait_ge(w_done, s + 1)
                        dve.wait_ge(up_mm, s + 1)
                        V.scalar_tensor_tensor(T[b], T[b], 0.5 * MLP_SCALE / (W_SCALE * W_SCALE), B[2 + b][:, :],
                                               ALU.mult, ALU.mult).then_inc(z_done, 1)
                        dve.wait_ge(zhi_done, s + 1)
                        V.tensor_tensor(zhl[:, b, 1, :], T[b], zhl[:, b, 0, :], ALU.subtract).then_inc(zlo_done, 1)
                        if unit:
                            dve.wait_ge(whi_done, c * UNITS + (UNITS + i + 1))
                            dstW = ffw[1 - par][:, :, th, nib, m, :]
                            V.tensor_tensor(dstW[:, 1], wf[:, i % 2, :], dstW[:, 0], ALU.subtract).then_inc(wlo_done, 1)
                        if ft == 0 and not (first and t == 0):
                            accumulate(c * NT + (t - 1), (t - 1) % NT)
                return k

            links[0] += chunk(0, 0, links[0], first=True)
            base = links[0]
            per = 2 * UNITS
            with dve.Fori(0, (NF - 2) // 2) as cp:
                assert chunk(cp * 2 + 1, 1, cp * (2 * per) + base) == per
                assert chunk(cp * 2 + 2, 0, cp * (2 * per) + (base + per)) == per
            chunk(NF - 1, 1, 0, last=True)
            accumulate(NF * NT - 1, NT - 1)

        @block.tensor
        def _(pe):
            T_ = nc.tensor

            def mod_row_mm(j):
                pe.wait_ge(colsum_done, j + 1)
                if j >= 2:
                    pe.wait_ge(mod_row, j - 1)
                T_.matmul(B[6 + j % 2][:, :], ones[:, :], colsum[j % 2], start=True, stop=True).then_inc(mod_mm, 1)

            def ln_transpose(ln, m, bank_free):
                pe.wait_ge(ht_done[ln], m + 1)
                for s_, v_ in bank_free:
                    pe.wait_ge(s_, v_)
                for k in range(KT):
                    if ln == 0:
                        src = ht[0][:, k * P:(k + 1) * P]
                    else:
                        src = ht[1][:, :].rearrange("p (j q two) -> p j two q", j=2, two=2)[:, k // 2, k % 2, :]
                    ins = T_.transpose(B[(5, 7)[ln]][:, k * P:(k + 1) * P], src, ident[:, :])
                ins.then_inc(lt_done[ln], 1)

            def three(out_, whi, wlo, mhi, mlo, start, stop):
                T_.matmul(out_, whi, mhi, start=start, stop=False)
                T_.matmul(out_, whi, mlo, start=False, stop=False)
                return T_.matmul(out_, wlo, mhi, start=False, stop=stop)

            def qk_tile(g, i):
                b = i % 4
                if i >= 4:
                    pe.wait_ge(qk_done, g * 8 + i - 3)
                j, ct = i % 2, i // 2
                for k in range(KT):
                    col = j * D + ct * P
                    ins = three(B[b][:, :], wqkv_hl[:, 0, k, col:col + P], wqkv_hl[:, 1, k, col:col + P],
                                h1_hl[:, 0, k, :], h1_hl[:, 1, k, :], k == 0, k == KT - 1)
                ins.then_inc(qk_mm, 1)

            def v_tile(g, c):
                pe.wait_ge(qk_done, g * 8 + 5 + c)
                for k in range(KT):
                    ins = three(B[c][:, :], h1_hl[:, 0, k, c * C:(c + 1) * C], h1_hl[:, 1, k, c * C:(c + 1) * C],
                                wqkv_hl[:, 0, k, 2 * D:3 * D], wqkv_hl[:, 1, k, 2 * D:3 * D], k == 0, k == KT - 1)
                ins.then_inc(v_mm, 1)

            def att_transpose(n, ln2_before):
                pe.wait_ge(att_done, n + 1)
                wait(pe, hhi_done[1], ln2_before)
                wait(pe, hlo_done[1], ln2_before)
                for k in range(KT):
                    ins = T_.transpose(B[7][:, k * P:(k + 1) * P], att[:, k * P:(k + 1) * P], ident[:, :])
                ins.then_inc(at_mm, 1)

            def out_proj(n):
                pe.wait_ge(ahi_done, n + 1)
                pe.wait_ge(alo_done, n + 1)
                pe.wait_ge(kd_done, n + 1)
                for k in range(KT):
                    a = att_hl[:, :, k * P:(k + 1) * P]
                    ins = three(B[4][:, :], a[:, 0, :], a[:, 1, :], wo_hl[:, 0, k, :], wo_hl[:, 1, k, :], k == 0, k == KT - 1)
                ins.then_inc(wo_mm, 1)

            def ln2(m, att_before):
                ln_transpose(1, m, [(ahi_done, att_before), (alo_done, att_before)])

            mod_row_mm(0)
            mod_row_mm(1)
            for m in range(GC):
                ln_transpose(0, m, [(hhi_done[0], m), (hlo_done[0], m)] if m else [])
            pe.wait_ge(wq_hi, 3 * KT)
            pe.wait_ge(wq_lo, 3 * KT)

            def slot(g, c, last):
                n = g * GC + c
                if c == 0:
                    pe.wait_ge(qk_done, g * 8 + 8)
                    wait(pe, x1_done, n)
                elif c > 1:
                    pe.wait_ge(x1_done, n - 1)
                else:
                    pe.wait_ge(kd_done, n)
                for k in range(KT):
                    ins = T_.transpose(B[4][:, k * P:(k + 1) * P], kT[:, k, c * C:(c + 1) * C], ident[:, :])
                ins.then_inc(kt_mm, 1)
                if c == 0:
                    pe.wait_ge(v_done, n + GC)
                for r in range(R):
                    rows = slice(HD * r, HD * r + HD)
                    for k in range(KT):
                        ins = T_.matmul(B[r][:, k * C:(k + 1) * C], kT[rows, k, c * C:(c + 1) * C],
                                        qT[rows, k, c * C:(c + 1) * C], start=True, stop=True)
                    ins.then_inc(sc_mm, 1)
                if c > 0:
                    att_transpose(n - 1, n - 1 if c == 1 else n - 2)
                pe.wait_ge(kd_done, n + 1)
                if not last:
                    pe.wait_ge(hhi_done[0], n + GC)
                    pe.wait_ge(hlo_done[0], n + GC)
                elif c > 0:
                    pe.wait_ge(snew_done, n)
                else:
                    pe.wait_ge(hhi_done[0], NCH)
                    pe.wait_ge(hlo_done[0], NCH)
                for k in range(KT):
                    ins = T_.matmul(B[5][:, k * P:(k + 1) * P], kd[:, k * P:(k + 1) * P],
                                    vv[:, c, k * P:(k + 1) * P], start=True, stop=True)
                ins.then_inc(st_mm, 1)
                if c > 0:
                    out_proj(n - 1)
                pe.wait_ge(qd_done, n + 1)
                pe.wait_ge(S_done, n + 1)
                if c == 0:
                    wait(pe, att_done, n)
                for k in range(KT):
                    T_.matmul(B[6][:, k * P:(k + 1) * P], qd[:, k * P:(k + 1) * P], S[:, c % 2, k * P:(k + 1) * P],
                              start=(k == 0), stop=False, skip_group_check=True)
                for r in range(R):
                    pe.wait_ge(pr_done, R * n + r + 1)
                    for k in range(KT):
                        h0 = (R * k + r) * HD
                        ins = T_.matmul(B[6][:, h0:h0 + HD], pr_rg[:, r, k, :], vv[:, c, h0:h0 + HD], start=False,
                                        stop=(r == R - 1 and k == KT - 1), skip_group_check=True)
                ins.then_inc(av_mm, 1)
                if not last:
                    ln_transpose(0, n + GC, [(snew_done, n + 1)])
                if c > 1:
                    ln2(n - 2, n)

            def group(g, first=False, last=False):
                pe.wait_ge(hhi_done[0], g * GC + GC)
                pe.wait_ge(hlo_done[0], g * GC + GC)
                for i in range(8):
                    qk_tile(g, i)
                    if first and i < 4:
                        mod_row_mm(2 + i)
                    if not first:
                        if i == 0:
                            att_transpose(g * GC - 1, g * GC - 2)
                        if i == 1:
                            ln2(g * GC - 2, g * GC)
                        if i == 2:
                            out_proj(g * GC - 1)
                        if i == 6:
                            pe.wait_ge(hhi_done[1], g * GC - 1)
                            pe.wait_ge(hlo_done[1], g * GC - 1)
                            ln2(g * GC - 1, g * GC)
                for c in range(GC):
                    v_tile(g, c)
                if first:
                    pe.wait_ge(mask_done, R)
                    pe.wait_ge(mod_row, 6)
                    pe.wait_ge(wo_lo, KT)
                for c in range(GC):
                    slot(g, c, last)

            group(0, first=True)
            with pe.Fori(1, G - 1) as g:
                group(g)
            group(G - 1, last=True)

            def gate_up(c, par, t, ft, first_steps):
                s = c * STEPS + t * FT + ft
                for m, (sem_free, sem_out) in enumerate(((w_done, gate_mm), (z_done, up_mm))):
                    if not first_steps:
                        pe.wait_ge(sem_free, s - 1)
                    for k in range(KT):
                        w = ffw[par][:, :, k // 2, k % 2, m, ft * P:(ft + 1) * P]
                        ins = three(B[2 * m + ft % 2][:, :], w[:, 0, :], w[:, 1, :],
                                    h2hi[:, k, bass.ds(t * GT, GT)], h2lo[:, k, bass.ds(t * GT, GT)],
                                    k == 0, k == KT - 1)
                    ins.then_inc(sem_out, 1)

            def down(s, par, tile_no, ft, first_tile=False):
                pe.wait_ge(zhi_done, s + 1)
                pe.wait_ge(zlo_done, s + 1)
                for q in range(GC):
                    if ft == 0 and not first_tile:
                        pe.wait_ge(acc_done, tile_no * GC + (q + 1 - GC))
                    z = zhl[:, ft % 2, :, q * P:(q + 1) * P]
                    w = ffw[par][:, :, ft // 2, ft % 2, 2, :]
                    ins = three(B[4 + q][:, :], z[:, 0, :], z[:, 1, :], w[:, 0, :], w[:, 1, :], ft == 0, ft == FT - 1)
                    ins.then_inc(dn_mm, 1)

            def weights_ready(c):
                pe.wait_ge(whi_done, c * UNITS + UNITS)
                pe.wait_ge(wlo_done, c * UNITS + UNITS)

            def chunk(c, par, first=False):
                weights_ready(c)
                s0 = c * STEPS
                for ft in range(FT):
                    if first and ft == 0:
                        pe.wait_ge(hhi_done[1], GC)
                        pe.wait_ge(hlo_done[1], GC)
                    gate_up(c, par, 0, ft, first and ft < 2)
                    if first and ft == 0:
                        att_transpose(NCH - 1, NCH - 2)
                        ln2(NCH - 2, NCH)
                        out_proj(NCH - 1)
                    elif first and ft == 1:
                        pe.wait_ge(hhi_done[1], NCH - 1)
                        pe.wait_ge(hlo_done[1], NCH - 1)
                        ln2(NCH - 1, NCH)
                        pe.wait_ge(hhi_done[1], NCH)
                        pe.wait_ge(hlo_done[1], NCH)
                        down(s0, par, 0, 0, first_tile=True)
                    elif ft == 0:
                        down(s0 - 1, 1 - par, c * NT - 1, FT - 1)
                    else:
                        down(s0 + ft - 1, par, c * NT, ft - 1)
                with pe.Fori(1, NT) as t:
                    for ft in range(FT):
                        gate_up(c, par, t, ft, False)
                        s = s0 + t * FT + ft
                        if ft == 0:
                            down(s - 1, par, c * NT + t - 1, FT - 1)
                        else:
                            down(s - 1, par, c * NT + t, ft - 1)

            chunk(0, 0, first=True)
            with pe.Fori(0, (NF - 2) // 2) as cp:
                chunk(cp * 2 + 1, 1)
                chunk(cp * 2 + 2, 0)
            chunk(NF - 1, 1)
            down(NF * STEPS - 1, 1, NF * NT - 1, FT - 1)


def kernel(**inputs):
    import numpy as np
    import concourse.bacc as bacc
    from concourse.bass_utils import run_bass_kernel_spmd

    a = {name: np.asarray(v) for name, v in inputs.items()}

    def up_codes(w):
        w = w.reshape(NF, 2, P, 2, 2, P)
        return w.transpose(0, 4, 5, 1, 3, 2).reshape(NF, 2, P, FC)

    def up_scales(s):
        s = s.reshape(NF, 2, P, 2, 2, 8)
        return s.transpose(0, 4, 5, 1, 3, 2).reshape(NF, 2, 8, FC)

    codes = np.stack([up_codes(a["L0_ffn_gate_W_packed"]), up_codes(a["L0_ffn_up_W_packed"]),
                      a["L0_ffn_down_W_packed"].reshape(D, NF, 2, P).transpose(1, 2, 3, 0)], axis=3)
    scales = np.stack([up_scales(a["L0_ffn_gate_scales"]), up_scales(a["L0_ffn_up_scales"]),
                       a["L0_ffn_down_scales"].reshape(D, NF, 2, 8).transpose(1, 2, 3, 0)], axis=3)
    arrays = {
        "x": a["L0_attn_x"].reshape(N, D), "wmod": a["L0_wmod"], "cond": a["L0_c"].reshape(KT, P).T,
        "wqkv": a["L0_attn_Wqkv"], "bqkv": a["L0_attn_bqkv"],
        "bqk_cols": a["L0_attn_bqkv"][0:2 * D].reshape(2 * KT, P).T, "wout": a["L0_attn_Wout"],
        "bout": a["L0_attn_bout"], "slopes": a["L0_attn_slopes"],
        "slopes_rg": a["L0_attn_slopes"].reshape(KT, R).T, "codes": codes, "scales": scales,
    }
    arrays = {name: np.ascontiguousarray(v) for name, v in arrays.items()}
    nc = bacc.Bacc("TRN2", target_bir_lowering=False, num_devices=1)
    aps = {name: nc.dram_tensor(name, v.shape, mybir.dt.from_np(v.dtype), kind="ExternalInput").ap()
           for name, v in arrays.items()}
    out = nc.dram_tensor("out", (N, D), F32, kind="ExternalOutput").ap()
    adaln_block_kernel(nc, out=out, **aps)
    r = run_bass_kernel_spmd(nc, [arrays], core_ids=[0])
    return r.results[0]["out"].reshape(1, N, D)
```

```python
from contextlib import ExitStack

import concourse.bass as bass
from concourse import mybir

F32 = mybir.dt.float32
F16 = mybir.dt.float16
I32 = mybir.dt.int32
ALU = mybir.AluOpType
ACT = mybir.ActivationFunctionType

P = 128
N = 2048
D = 512
KT = D // P
H = 16
HD = D // H
R = P // HD
C = P
NCH = N // C
GC = 4
G = NCH // GC
GT = GC * C
F = 4096
FC = 512
NF = F // FC
FT = FC // P
NT = N // GT
STEPS = NT * FT
UNITS = 12
EPS = 1e-5

W_SCALE = 2.0 ** 8
ATT_SCALE = 2.0 ** -4
MLP_SCALE = 2.0 ** -3
CODE_SCALE = 2.0 ** 14
CODE_MASK = 0x8E000000 - (1 << 32)
GELU_A = 0.7978845608028654
GELU_B = 0.044715


def adaln_block_kernel(nc, x, wmod, cond, wqkv, bqkv, bqk_cols, wout, bout, slopes, slopes_rg, codes, scales, out):
    with ExitStack() as ctx:
        def sb(name, shape, dt=F32):
            return ctx.enter_context(nc.sbuf_tensor(name, shape, dt))

        def sem(name):
            return ctx.enter_context(nc.semaphore(name))

        xs = sb("xs", [P, NCH * D])
        h2 = sb("h2", [P, 2 * KT * N], F16)
        h2hi = h2[:, 0:KT * N].rearrange("p (k t) -> p k t", k=KT)
        h2lo = h2[:, KT * N:2 * KT * N].rearrange("p (k t) -> p k t", k=KT)
        h2_f32 = h2[:, :].bitcast(F32)
        wq_in = [h2_f32[:, j * 2048:(j + 1) * 2048].rearrange("p (k n) -> p k n", k=KT) for j in range(3)]
        wo_in = h2_f32[:, 6144:8192].rearrange("p (k n) -> p k n", k=KT)

        wa = sb("wa", [P, 2 * KT * 3 * D], F16)
        wqkv_hl = wa[:, :].rearrange("p (j s k n) -> p j s k n", j=3, s=2, k=KT)
        qkv = sb("qkv", [P, 3 * KT * GT])
        qT = qkv[:, 0:2048].rearrange("p (g t) -> p g t", g=KT)
        kT = qkv[:, 2048:4096].rearrange("p (g t) -> p g t", g=KT)
        vv = qkv[:, 4096:6144].rearrange("p (c n) -> p c n", c=GC)
        wb = qkv[:, :].bitcast(F16)
        ffw = [w.rearrange("p (t b s m n) -> p t b s m n", t=2, b=2, s=2, m=3) for w in (wa[:, :], wb)]

        wo = sb("wo", [P, 2 * KT * D], F16)
        wo_hl = wo[:, :].rearrange("p (s k n) -> p s k n", s=2, k=KT)
        h1 = sb("h1", [P, 2 * KT * GT], F16)
        h1_hl = h1[:, :].rearrange("p (s k t) -> p s k t", s=2, k=KT)

        stage = sb("stage", [P, 4608])
        wm_in = [stage[:, j * 2048:(j + 1) * 2048].rearrange("p (k n) -> p k n", k=KT) for j in range(2)]
        pk = stage[:, 0:3072].bitcast(I32).rearrange("p (t m n) -> p t m n", t=2, m=3)
        scl = [stage[:, 3072:4608].rearrange("p (m n) -> p m n", m=3),
               h1[:, 0:3072].bitcast(F32).rearrange("p (m n) -> p m n", m=3)]

        mask = sb("mask", [P, R * KT * C])
        mask_r = mask[:, :].rearrange("p (r n) -> p r n", r=R)
        pr = sb("pr", [P, R * KT * C])
        pr_r = pr[:, :].rearrange("p (r n) -> p r n", r=R)
        pr_rg = pr[:, :].rearrange("p (r g i) -> p r g i", r=R, g=KT)
        colsum = [pr[:, j * D:(j + 1) * D] for j in range(2)]
        gt = [pr[:, 2 * D:3 * D], pr[:, 3 * D:4 * D]]
        T = [mask[:, j * D:(j + 1) * D] for j in range(2)]
        zhl = pr[:, 0:2 * D].bitcast(F16).rearrange("p (b s n) -> p b s n", b=2, s=2)

        qdec = sb("qdec", [P, KT * C])
        kdec = sb("kdec", [P, H])
        sdec = sb("sdec", [P, D])
        bmask = sb("bmask", [P, D])
        kd = sb("kd", [P, D])
        qd = sb("qd", [P, KT * C])
        S = sb("S", [P, 2, D])
        s_dec = sb("s_dec", [P, D])
        s_new = sb("s_new", [P, D])
        ga_bc = sb("ga_bc", [P, D])
        att_hl = sb("att_hl", [P, 2, D], F16)
        ht = [sb("ht1", [P, D]), sb("ht2", [P, D])]
        ht_first = [ht[0], ht[1], kd, qd]
        xint = sb("xint", [P, D], I32)
        sca = sb("sca", [P, 2, D])
        wf = sca
        sa_bc, ca_bc = sca[:, 0, :], sca[:, 1, :]
        sb_bc, cb_bc, gb_bc = (sb(n, [P, D]) for n in ("sb_bc", "cb_bc", "gb_bc"))
        bga = sb("bga", [P, D])
        bv_bc = sb("bv_bc", [P, D])
        ident = sb("ident", [P, P])
        ones = sb("ones", [P, P])
        dif = s_new[:, 0:P].bitcast(I32)
        difc = gt[0][:, 0:P]
        ge = gt[0][:, P:2 * P]
        idx = gt[0][:, 2 * P:3 * P]
        small = sb("small", [P, 144])
        cT, ce, c1, sil = (small[:, 4 * j:4 * j + 4] for j in range(4))
        spart = small[:, 16:20]
        nsp = small[:, 20:24]
        bdec = small[:, 24:28]
        bqk = small[:, 28:36]
        nsl = small[:, 36:52]
        cj = small[:, 52:53]
        epow4 = small[:, 96:100]
        epow = epow4[:, 0:1]
        epsc4 = small[:, 100:104]
        epsc = epsc4[:, 0:1]
        mv4 = small[:, 104:112]
        stat4 = small[:, 120:144]
        ve4, rs4 = small[:, 112:116], small[:, 116:120]
        stat = [small[:, 54:60], small[:, 60:66]]
        mv = [small[:, 66:68], small[:, 68:70]]
        ve = [small[:, 70:71], small[:, 71:72]]
        rs = [small[:, 72:73], small[:, 73:74]]
        slp = small[:, 76:92]
        tick = small[:, 92:93]
        ints = sb("ints", [P, 1], I32)
        idxi = xint[:, 0:P]

        B = [ctx.enter_context(nc.psum_tensor(f"bank{b}", [P, 512], F32)) for b in range(8)]

        in_small, in_wmod0, in_wmod1, in_x0, in_x, in_wout = (
            sem(n) for n in ("in_small", "in_wmod0", "in_wmod1", "in_x0", "in_x", "in_wout"))
        in_cond = sem("in_cond")
        in_wmod = [in_wmod0, in_wmod1]
        in_wq = [sem(f"in_wq{j}") for j in range(3)]
        in_half = [sem("in_half0"), sem("in_half1")]
        out_done = sem("out_done")
        iota_done, const_done, exp_done, mask_done, sdec_done = (
            sem(n) for n in ("iota_done", "const_done", "exp_done", "mask_done", "sdec_done"))
        silu_exp, silu_done, colsum_done, mod_mm, mod_row, gates_done = (
            sem(n) for n in ("silu_exp", "silu_done", "colsum_done", "mod_mm", "mod_row", "gates_done"))
        wq_hi, wq_lo, wo_f, wo_hi, wo_lo = (sem(n) for n in ("wq_hi", "wq_lo", "wo_f", "wo_hi", "wo_lo"))
        dve_chain, pool_chain = sem("dve_chain"), sem("pool_chain")
        stats_done = [sem("stats1_done"), sem("stats2_done")]
        rstd_done = [sem("rstd1_done"), sem("rstd2_done")]
        norm_done = [sem("norm1_done"), sem("norm2_done")]
        ht_done = [sem("ht1_done"), sem("ht2_done")]
        lt_done = [sem("lt1_done"), sem("lt2_done")]
        hhi_done = [sem("h1hi_done"), sem("h2hi_done")]
        hlo_done = [sem("h1lo_done"), sem("h2lo_done")]
        xb_done, x1_done = sem("xb_done"), sem("x1_done")
        qk_mm, qk_done, v_mm, v_done = (sem(n) for n in ("qk_mm", "qk_done", "v_mm", "v_done"))
        kt_mm, kd_done, sc_mm, pr_done = (sem(n) for n in ("kt_mm", "kd_done", "sc_mm", "pr_done"))
        st_mm, snew_done, sdecay_done, S_done, qd_done = (
            sem(n) for n in ("st_mm", "snew_done", "sdecay_done", "S_done", "qd_done"))
        av_mm, ahi_done, alo_done, wo_mm = (sem(n) for n in ("av_mm", "ahi_done", "alo_done", "wo_mm"))
        stats4_done, rstd4_done, norm3_done, ht3_done, ht012_done = (
            sem(n) for n in ("stats4_done", "rstd4_done", "norm3_done", "ht3_done", "ht012_done"))
        wf_done, whi_done, wlo_done = (sem(n) for n in ("wf_done", "whi_done", "wlo_done"))
        gate_mm, up_mm, dn_mm = (sem(n) for n in ("gate_mm", "up_mm", "dn_mm"))
        sq_done, u_done, th_done, w_done, z_done, zhi_done, zlo_done, acc_done = (
            sem(n) for n in ("sq_done", "u_done", "th_done", "w_done", "z_done", "zhi_done", "zlo_done", "acc_done"))

        block = ctx.enter_context(nc.Block())

        def wait(eng, s_, v_):
            if not (isinstance(v_, int) and v_ <= 0):
                eng.wait_ge(s_, v_)

        def xrow(n):
            return xs[:, bass.ds(n * D, D)]

        def count(ln, n):
            return n + 1 - (GC if ln == 0 else 0)

        MODS = ["sa", "ca", "ga", "sb", "cb", "gb"]
        SETUP = [0, 1, 2, 3, 4, 5]

        def chunk0_unit(U):
            return ffw[0][:, U // 6, U // 3 % 2, :, U % 3, :]

        def chunk0_slot(c):
            return range(6 + 2 * c, 8 + 2 * c) if c < 3 else ()

        @block.sync
        def _(sp):
            sp.dma_start(cT, cond).then_inc(in_cond, 16)
            wm = wmod.rearrange("(k p) (s n) -> p k s n", p=P, s=6)

            def load_wmod(j):
                if j >= 2:
                    sp.wait_ge(colsum_done, j - 1)
                sp.dma_start(wm_in[j % 2], wm[:, :, SETUP[j], :]).then_inc(in_wmod[j % 2], 16)

            xv = x.rearrange("(g c p) n -> g p c n", p=P, c=GC)
            load_wmod(0)
            load_wmod(1)
            sp.dma_start(xs[:, 0:GC * D].rearrange("p (c n) -> p c n", c=GC), xv[0]).then_inc(in_x0, 16)
            for r in range(R):
                sp.dma_start(spart[HD * r:HD * r + HD, :],
                             slopes_rg[r:r + 1, :].to_broadcast([HD, KT])).then_inc(in_small, 16)
            row = slopes.rearrange("(a n) -> a n", a=1)
            sp.dma_start(slp, row.to_broadcast([P, H])).then_inc(in_small, 16)
            sp.dma_start(bqk, bqk_cols).then_inc(in_small, 16)
            brow = bqkv.rearrange("(a n) -> a n", a=1)
            sp.dma_start(bv_bc[:, :], brow[:, 2 * D:3 * D].to_broadcast([P, D])).then_inc(in_small, 16)
            sp.dma_start(bga[:, :], bout.rearrange("(a n) -> a n", a=1).to_broadcast([P, D])).then_inc(in_small, 16)
            wqv = wqkv.rearrange("(k p) (j n) -> j p k n", p=P, j=3)
            for j in range(3):
                sp.dma_start(wq_in[j], wqv[j]).then_inc(in_wq[j], 16)
            for j in range(2, 6):
                load_wmod(j)
            sp.dma_start(wo_in, wout.rearrange("(k p) n -> p k n", p=P)).then_inc(in_wout, 16)
            for g in range(1, G):
                sp.dma_start(xs[:, g * GC * D:(g + 1) * GC * D].rearrange("p (c n) -> p c n", c=GC),
                             xv[g]).then_inc(in_x, 16)

            def load_half(c, t):
                sp.dma_start(pk[:, t, :, :], codes[bass.ds(c, 1), t].rearrange("a p m n -> (a p) m n")).then_inc(in_half[t], 16)
                src = scales[bass.ds(c, 1), t].rearrange("a b m n -> (a b) (m n)").unsqueeze(1)
                sp.dma_start(scl[t].rearrange("p m n -> p (m n)"),
                             src.to_broadcast([8, 16, 3 * D])).then_inc(in_half[t], 16)

            sp.wait_ge(colsum_done, 6)
            load_half(0, 0)
            sp.wait_ge(v_mm, NCH)
            load_half(0, 1)
            with sp.Fori(1, NF) as c:
                for t in range(2):
                    sp.wait_ge(wf_done, c * UNITS - UNITS + 6 * (t + 1))
                    load_half(c, t)
            ov = out.rearrange("(n p) d -> n p d", p=P)
            for n in range(NCH):
                sp.wait_ge(acc_done, NCH * (NF - 1) + n + 1)
                sp.dma_start(ov[n], xs[:, n * D:(n + 1) * D]).then_inc(out_done, 16)
            sp.wait_ge(out_done, 16 * NCH)

        @block.gpsimd
        def _(pool):
            nc.gpsimd.iota(dif, pattern=[[1, P]], base=0, channel_multiplier=-1).then_inc(iota_done, 1)
            nc.gpsimd.iota(idxi, pattern=[[1, P]], base=0, channel_multiplier=0).then_inc(iota_done, 1)
            nc.gpsimd.iota(ints[:, :], pattern=[[1, 1]], base=C, channel_multiplier=-1).then_inc(iota_done, 1)
            nc.gpsimd.memset(epow4, -0.5)
            nc.gpsimd.memset(epsc4, EPS).then_inc(pool_chain, 1)
            chain = [1]

            def rstd(ln, n, base):
                pool.wait_ge(stats_done[ln], count(ln, n))
                nc.gpsimd.tensor_tensor(ve[ln], mv[ln][:, 1:2], epsc, ALU.add).then_inc(pool_chain, 1)
                pool.wait_ge(pool_chain, base + 1)
                nc.gpsimd.tensor_tensor(rs[ln], ve[ln], epow, ALU.pow).then_inc(rstd_done[ln], 1)

            def modulate(ln, n, base):
                pool.wait_ge(norm_done[ln], count(ln, n))
                nc.gpsimd.tensor_tensor(ht[ln][:, :], ht[ln][:, :], (ca_bc, cb_bc[:, :])[ln], ALU.mult).then_inc(pool_chain, 1)
                pool.wait_ge(pool_chain, base + 1)
                nc.gpsimd.tensor_tensor(ht[ln][:, :], ht[ln][:, :], (sa_bc, sb_bc[:, :])[ln], ALU.add).then_inc(ht_done[ln], 1)

            def layer_norm(ln, n, base):
                rstd(ln, n, base)
                modulate(ln, n, base + 1)

            def add_bias(m):
                nc.gpsimd.tensor_tensor(xrow(m), xrow(m), bga[:, :], ALU.add).then_inc(xb_done, 1)

            def slot(n, c, base, lo_ln1, lo_ln2):
                if c == 0:
                    pool.wait_ge(qk_done, (n + GC) * 2)
                wait(pool, av_mm, n)
                nc.gpsimd.tensor_tensor(qd[:, :].rearrange("p (g i) -> p g i", g=KT), qT[:, :, c * C:(c + 1) * C],
                                        qdec[:, :].rearrange("p (g i) -> p g i", g=KT), ALU.mult).then_inc(qd_done, 1)
                pool.wait_ge(S_done, n + 1)
                nc.gpsimd.tensor_tensor(s_dec[:, :], S[:, c % 2, :], sdec[:, :], ALU.mult).then_inc(sdecay_done, 1)
                k = 0
                if lo_ln1:
                    layer_norm(0, n + GC, base + k)
                    add_bias(n + GC)
                    k += 2
                if lo_ln2:
                    layer_norm(1, n - 1, base + k)
                    k += 2
                return k

            pool.wait_ge(pool_chain, 1)
            pool.wait_ge(stats4_done, 1)
            nc.gpsimd.tensor_tensor(ve4, mv4.rearrange("p (c two) -> p two c", two=2)[:, 1, :], epsc4,
                                    ALU.add).then_inc(pool_chain, 1)
            pool.wait_ge(pool_chain, 2)
            nc.gpsimd.tensor_tensor(rs4, ve4, epow4, ALU.pow).then_inc(rstd4_done, 1)
            pool.wait_ge(mod_row, 2)
            pool.wait_ge(norm3_done, 1)
            h3 = ht_first[3][:, :]
            nc.gpsimd.tensor_tensor(h3, h3, ca_bc, ALU.mult).then_inc(pool_chain, 1)
            pool.wait_ge(pool_chain, 3)
            nc.gpsimd.tensor_tensor(h3, h3, sa_bc, ALU.add).then_inc(ht3_done, 1)
            chain[0] += 2
            pool.wait_ge(gates_done, 2)
            for m in range(GC):
                add_bias(m)
            pool.wait_ge(sdec_done, 1)

            def group(g, base, first=False, last=False):
                k = 0
                if not first:
                    layer_norm(1, g * GC - 1, base)
                    k += 2
                for c in range(GC):
                    k += slot(g * GC + c, c, base + k, not last, c > 0)
                return k

            pool.wait_ge(mod_row, 6)
            chain[0] += group(0, chain[0], first=True)
            per = 2 + 2 * GC + 2 * (GC - 1)
            base = chain[0]
            with pool.Fori(1, G - 1) as g:
                assert group(g, (g - 1) * per + base) == per
            group(G - 1, base + (G - 2) * per, last=True)
            layer_norm(1, NCH - 1, base + (G - 2) * per + 2 + 2 * (GC - 1))

        @block.scalar
        def _(act):
            act.wait_ge(in_cond, 16)
            nc.scalar.activation(ce, cT, ACT.Exp, scale=-1.0).then_inc(silu_exp, 1)
            dst = {"sa": sa_bc, "ca": ca_bc, "ga": ga_bc[:, :], "sb": sb_bc[:, :], "cb": cb_bc[:, :], "gb": gb_bc[:, :]}

            def mod_rows(j):
                name = MODS[SETUP[j]]
                act.wait_ge(mod_mm, j + 1)
                nc.scalar.activation(dst[name], B[6 + j % 2][:, :], ACT.Identity,
                                     bias=ones[:, 0:1] if name in ("ca", "cb") else 0.0).then_inc(mod_row, 1)

            def split_hi(ln, m, col, bank=None):
                act.wait_ge(lt_done[ln], m + 1)
                dstT = h1_hl[:, 0, :, col:col + C] if ln == 0 else h2hi[:, :, bass.ds(col, C)]
                nc.scalar.copy(dstT, B[(5, 7)[ln] if bank is None else bank][:, :].rearrange("p (k t) -> p k t", k=KT)).then_inc(hhi_done[ln], 1)

            mod_rows(0)
            mod_rows(1)
            def wqkv_hi(j):
                act.wait_ge(in_wq[j], 16)
                for k in range(KT):
                    nc.scalar.activation(wqkv_hl[:, j, 0, k, :], wq_in[j][:, k, :], ACT.Copy,
                                         scale=W_SCALE).then_inc(wq_hi, 1)

            wqkv_hi(0)
            wqkv_hi(1)
            for m in range(GC):
                split_hi(0, m, m * C, bank=m)
            wqkv_hi(2)
            act.wait_ge(const_done, 1)
            nc.scalar.activation(bdec, nsp, ACT.Exp, scale=float(C)).then_inc(exp_done, 1)
            nc.scalar.activation(kdec[:, :], nsl, ACT.Exp, scale=cj).then_inc(exp_done, 1)
            for g in range(KT):
                nc.scalar.activation(qdec[:, g * C:(g + 1) * C], idx, ACT.Exp, scale=nsp[:, g:g + 1]).then_inc(exp_done, 1)
            for r in range(R):
                for g in range(KT):
                    h = R * g + r
                    nc.scalar.activation(mask_r[:, r, g * C:(g + 1) * C], difc, ACT.Exp,
                                         scale=nsl[:, h:h + 1]).then_inc(exp_done, 1)

            def att_hi(n):
                act.wait_ge(av_mm, n + 1)
                nc.scalar.activation(att_hl[:, 0, :], B[6][:, :], ACT.Copy, scale=ATT_SCALE).then_inc(ahi_done, 1)

            def qk_out(g, i):
                act.wait_ge(qk_mm, g * 8 + i + 1)
                dstT = (qT, kT)[i // KT][:, i % KT, :]
                nc.scalar.activation(dstT, B[i % 4][:, :], ACT.Identity, bias=bqk[:, i:i + 1],
                                     scale=1.0 / W_SCALE).then_inc(qk_done, 1)

            def weight_hi(U, dstW):
                act.wait_ge(wf_done, U + 1)
                nc.scalar.copy(dstW[:, 0], wf[:, U % 2, :]).then_inc(whi_done, 1)

            def group(g, first=False, last=False):
                if not first:
                    att_hi(g * GC - 1)
                for i in range(8):
                    qk_out(g, i)
                    if first and i > 4:
                        mod_rows(i - 3)
                    if not first:
                        if i == 0:
                            split_hi(1, g * GC - 2, (g * GC - 2) * C)
                        if i == 5:
                            split_hi(1, g * GC - 1, (g * GC - 1) * C)
                    if last and i == 4:
                        act.wait_ge(qk_mm, NCH * 2 - 4)
                        for U in range(3):
                            weight_hi(U, chunk0_unit(U))
                if first:
                    mod_rows(5)
                    for k in range(KT):
                        act.wait_ge(wo_f, k + 1)
                        nc.scalar.copy(wo_hl[:, 0, k, :], wo_in[:, k, :]).then_inc(wo_hi, 1)
                if last:
                    act.wait_ge(qk_mm, NCH * 2)
                    for U in range(3, 6):
                        weight_hi(U, chunk0_unit(U))
                for c in range(GC):
                    n = g * GC + c
                    if c > 0:
                        att_hi(n - 1)
                    if last:
                        for U in chunk0_slot(c):
                            act.wait_ge(v_mm, NCH)
                            weight_hi(U, chunk0_unit(U))
                    if not last:
                        split_hi(0, n + GC, c * C)
                    if c > 1:
                        split_hi(1, n - 2, (n - 2) * C)

            group(0, first=True)
            with act.Fori(1, G - 1) as g:
                group(g)
            group(G - 1, last=True)
            att_hi(NCH - 1)
            split_hi(1, NCH - 2, (NCH - 2) * C)
            split_hi(1, NCH - 1, (NCH - 1) * C)

            def chunk(c, par, first=False, last=False):
                for t in range(NT):
                    for ft in range(FT):
                        s = c * STEPS + (t * FT + ft)
                        b = ft % 2
                        act.wait_ge(gate_mm, s + 1)
                        if not (first and t == 0 and ft < 2):
                            act.wait_ge(zlo_done, s - 1)
                        nc.scalar.activation(T[b], B[b][:, :], ACT.Square, scale=1.0 / W_SCALE).then_inc(sq_done, 1)
                        act.wait_ge(u_done, s + 1)
                        nc.scalar.activation(T[b], T[b], ACT.Tanh, scale=GELU_A * GELU_B / W_SCALE).then_inc(th_done, 1)
                        if ft > 0 and not last:
                            th, nib, m = t // 2, t % 2, ft - 1
                            i = 3 * t + m
                            act.wait_ge(wf_done, c * UNITS + (UNITS + i + 1))
                            wait(act, dn_mm, c * (STEPS * GC))
                            nc.scalar.copy(ffw[1 - par][:, th, nib, 0, m, :], wf[:, i % 2, :]).then_inc(whi_done, 1)
                        act.wait_ge(z_done, s + 1)
                        if not (first and t == 0 and ft < 2):
                            act.wait_ge(dn_mm, c * (STEPS * GC) + GC * (t * FT + ft - 1))
                        nc.scalar.copy(zhl[:, b, 0, :], T[b]).then_inc(zhi_done, 1)

            chunk(0, 0, first=True)
            with act.Fori(0, (NF - 2) // 2) as cp:
                chunk(cp * 2 + 1, 1)
                chunk(cp * 2 + 2, 0)
            chunk(NF - 1, 1, last=True)

        @block.vector
        def _(dve):
            links = [0]

            def link(ins, base, k):
                ins.then_inc(dve_chain, 1)
                dve.wait_ge(dve_chain, base + k)

            def link0(ins):
                links[0] += 1
                link(ins, links[0], 0)

            V = nc.vector
            V.memset(ones[:, :], 1.0)
            link0(V.memset(bmask[:, :], 0.0))
            V.memset(S[:, 0, :], 0.0).then_inc(S_done, 1)
            for r in range(R):
                V.memset(bmask[HD * r:HD * r + HD, :].rearrange("p (g e) -> p g e", g=KT)[:, :, HD * r:HD * r + HD], 1.0)
            dve.wait_ge(iota_done, 3)
            V.tensor_scalar(ident[:, :], dif, 0.0, None, ALU.is_equal)
            V.tensor_scalar(difc, dif, 0.0, None, ALU.max)
            V.tensor_scalar(ge, dif, 0.0, None, ALU.is_ge)
            V.tensor_copy(idx, idxi)
            V.tensor_copy(cj, ints[:, :])
            dve.wait_ge(in_cond, 16)
            dve.wait_ge(silu_exp, 1)
            link0(V.tensor_scalar(c1, ce, 1.0, None, ALU.add))
            link0(V.reciprocal(ce, c1))
            link0(V.tensor_tensor(sil, cT, ce, ALU.mult))

            def mod_sum(j):
                dve.wait_ge(in_wmod[j % 2], 16 * (j // 2 + 1))
                if j >= 2:
                    dve.wait_ge(mod_mm, j - 1)
                w, t = wm_in[j % 2], colsum[j % 2]
                link0(V.tensor_scalar(t, w[:, 0, :], sil[:, 0:1], None, ALU.mult))
                for k in range(1, KT):
                    ins = V.scalar_tensor_tensor(t, w[:, k, :], sil[:, k:k + 1], t, ALU.mult, ALU.add)
                    if k < KT - 1:
                        link0(ins)
                ins.then_inc(colsum_done, 1)

            mod_sum(0)
            mod_sum(1)
            dve.wait_ge(in_small, 16 * 8)
            V.tensor_scalar(nsp, spart, -1.0, None, ALU.mult)
            V.tensor_scalar(nsl, slp, -1.0, None, ALU.mult).then_inc(const_done, 1)

            def stats(ln, n, base, k):
                V.bn_stats(stat[ln], xrow(n)).then_inc(dve_chain, 1)
                dve.wait_ge(dve_chain, base + k)
                V.memset(tick, 0.0)
                V.bn_aggr(mv[ln], stat[ln]).then_inc(stats_done[ln], 1)

            def normalise(ln, n):
                dve.wait_ge(rstd_done[ln], count(ln, n))
                wait(dve, lt_done[ln], n)
                V.tensor_scalar(ht[ln][:, :], xrow(n), mv[ln][:, 0:1], rs[ln], ALU.subtract,
                                ALU.mult).then_inc(norm_done[ln], 1)

            def split_lo(ln, m, col, bank=None):
                dve.wait_ge(hhi_done[ln], m + 1)
                dstT = (h1_hl[:, :, :, col:col + C] if ln == 0 else None)
                hi = dstT[:, 0] if ln == 0 else h2hi[:, :, bass.ds(col, C)]
                lo = dstT[:, 1] if ln == 0 else h2lo[:, :, bass.ds(col, C)]
                V.tensor_tensor(lo, B[(5, 7)[ln] if bank is None else bank][:, :].rearrange("p (k t) -> p k t", k=KT), hi,
                                ALU.subtract).then_inc(hlo_done[ln], 1)

            def wq_split(j):
                for k in range(KT):
                    dve.wait_ge(wq_hi, j * KT + k + 1)
                    V.scalar_tensor_tensor(wqkv_hl[:, j, 1, k, :], wq_in[j][:, k, :], W_SCALE,
                                           wqkv_hl[:, j, 0, k, :], ALU.mult, ALU.subtract).then_inc(wq_lo, 1)

            dve.wait_ge(in_x0, 16)
            for m in range(GC):
                ins = V.bn_stats(stat4[:, 6 * m:6 * m + 6], xrow(m))
            link0(ins)
            for m in range(GC):
                ins = V.bn_aggr(mv4[:, 2 * m:2 * m + 2], stat4[:, 6 * m:6 * m + 6])
            ins.then_inc(stats4_done, 1)
            dve.wait_ge(rstd4_done, 1)
            for m in (3, 0, 1, 2):
                h = ht_first[m][:, :]
                ins = V.tensor_scalar(h, xrow(m), mv4[:, 2 * m:2 * m + 1], rs4[:, m:m + 1], ALU.subtract, ALU.mult)
                if m == 3:
                    ins.then_inc(norm3_done, 1)
                    dve.wait_ge(mod_row, 2)
                    continue
                link0(ins)
                link0(V.tensor_tensor(h, h, ca_bc, ALU.mult))
                V.tensor_tensor(h, h, sa_bc, ALU.add).then_inc(ht012_done, 1)
            wq_split(0)
            for m in range(GC):
                split_lo(0, m, m * C, bank=m)
            wq_split(1)
            wq_split(2)
            for j in range(2, 6):
                mod_sum(j)
            dve.wait_ge(exp_done, 6 + R * KT)
            for r in range(R):
                m3 = mask_r[:, r, :].rearrange("p (g i) -> p g i", g=KT)
                V.tensor_tensor(m3, m3, ge.unsqueeze(1).to_broadcast([P, KT, C]), ALU.mult).then_inc(mask_done, 1)
            for g in range(KT):
                ins = V.tensor_scalar(sdec[:, g * C:(g + 1) * C], bmask[:, g * C:(g + 1) * C], bdec[:, g:g + 1],
                                      None, ALU.mult)
            ins.then_inc(sdec_done, 1)

            def guard(g_bc):
                V.tensor_scalar(gt[0], g_bc[:, :], 0.0, 2.0, ALU.is_ge, ALU.mult)
                link0(V.scalar_tensor_tensor(gt[1], g_bc[:, :], -1.0, g_bc[:, :], ALU.mult, ALU.max))
                link0(V.tensor_scalar(gt[1], gt[1], 0.25, None, ALU.max))
                return V.scalar_tensor_tensor(g_bc[:, :], gt[0], -1.0, gt[1], ALU.add, ALU.mult)

            dve.wait_ge(mask_done, R)
            dve.wait_ge(mod_row, 3)
            guard(ga_bc).then_inc(gates_done, 1)
            dve.wait_ge(gates_done, 1)
            V.tensor_tensor(bga[:, :], bga[:, :], ga_bc[:, :], ALU.mult).then_inc(gates_done, 1)
            dve.wait_ge(in_wout, 16)
            for k in range(KT):
                V.scalar_tensor_tensor(wo_in[:, k, :], wo_in[:, k, :], W_SCALE, ga_bc[:, :], ALU.mult,
                                       ALU.mult).then_inc(wo_f, 1)
            dve.wait_ge(mod_row, 6)
            guard(gb_bc).then_inc(gates_done, 1)
            dve.wait_ge(gates_done, 3)

            def att_lo(n):
                dve.wait_ge(ahi_done, n + 1)
                V.scalar_tensor_tensor(att_hl[:, 1, :], B[6][:, :], ATT_SCALE, att_hl[:, 0, :], ALU.mult,
                                       ALU.subtract).then_inc(alo_done, 1)

            def residual(n, k0, base):
                dve.wait_ge(wo_mm, n + 1)
                dve.wait_ge(xb_done, n + 1)
                V.scalar_tensor_tensor(xrow(n), B[4][:, :], 1.0 / (W_SCALE * ATT_SCALE), xrow(n), ALU.mult,
                                       ALU.add).then_inc(x1_done, 1)
                dve.wait_ge(x1_done, n + 1)
                V.memset(tick, 0.0)
                stats(1, n, base, k0)

            def v_out(g, c):
                dve.wait_ge(v_mm, g * GC + c + 1)
                V.scalar_tensor_tensor(vv[:, c, :], B[c][:, :], 1.0 / W_SCALE, bv_bc[:, :], ALU.mult,
                                       ALU.add).then_inc(v_done, 1)

            def decode(i, th, nib, m, k, base):
                codes_t = pk[:, th, m, :]
                sc_t = scl[th][:, m, :]
                if m == 2 and nib == 0:
                    V.tensor_tensor(sc_t, sc_t, gb_bc[:, :], ALU.mult)
                link(V.tensor_scalar(xint[:, :], codes_t, 28 - 4 * nib, 3, ALU.logical_shift_left,
                                     ALU.arith_shift_right), base, k + 1)
                link(V.tensor_scalar(xint[:, :], xint[:, :], CODE_MASK, None, ALU.bitwise_and), base, k + 2)
                val = xint[:, :].bitcast(F16).rearrange("p (n two) -> p n two", two=2)[:, :, 1]
                V.scalar_tensor_tensor(wf[:, i % 2, :], val, CODE_SCALE * W_SCALE, sc_t, ALU.mult,
                                       ALU.mult).then_inc(wf_done, 1)
                return 2

            def weight_lo(U, i, dstW):
                dve.wait_ge(whi_done, U + 1)
                V.tensor_tensor(dstW[:, 1], wf[:, i % 2, :], dstW[:, 0], ALU.subtract).then_inc(wlo_done, 1)

            def chunk0(U, k, base):
                wait(dve, wf_done, U)
                used = decode(U, U // 6, U // 3 % 2, U % 3, k, base)
                if U > 0:
                    weight_lo(U - 1, U - 1, chunk0_unit(U - 1))
                return used

            def slot(n, c, base, last):
                k = 0
                if not last:
                    k += 1
                    stats(0, n + GC, base, k)
                dve.wait_ge(kt_mm, n + 1)
                V.tensor_tensor(kd[:, :].rearrange("p (h d) -> p h d", h=H), B[4][:, :].rearrange("p (h d) -> p h d", h=H),
                                kdec[:, :].unsqueeze(2).to_broadcast([P, H, HD]), ALU.mult).then_inc(kd_done, 1)
                for r in range(R):
                    dve.wait_ge(sc_mm, R * n + r + 1)
                    V.tensor_tensor(pr_r[:, r, :], B[r][:, :], mask_r[:, r, :], ALU.mult).then_inc(pr_done, 1)
                    if r == 1:
                        if not last:
                            normalise(0, n + GC)
                        if c > 0:
                            att_lo(n - 1)
                dve.wait_ge(st_mm, n + 1)
                V.tensor_tensor(s_new[:, :], B[5][:, :], bmask[:, :], ALU.mult).then_inc(snew_done, 1)
                dve.wait_ge(snew_done, n + 1)
                dve.wait_ge(sdecay_done, n + 1)
                V.tensor_tensor(S[:, (c + 1) % 2, :], s_dec[:, :], s_new[:, :], ALU.add).then_inc(S_done, 1)
                if c > 0:
                    k += 1
                    residual(n - 1, k, base)
                if last:
                    if c == 0:
                        dve.wait_ge(in_half[1], 32)
                    for U in chunk0_slot(c):
                        k += chunk0(U, k, base)
                    if c == 2:
                        weight_lo(UNITS - 1, UNITS - 1, chunk0_unit(UNITS - 1))
                if not last:
                    split_lo(0, n + GC, c * C)
                if c > 0:
                    normalise(1, n - 1)
                if c > 1:
                    split_lo(1, n - 2, (n - 2) * C)
                return k

            def group(g, base, first=False, last=False):
                k = 0
                if not first:
                    p3 = g * GC - 1
                    att_lo(p3)
                    split_lo(1, p3 - 1, (p3 - 1) * C)
                    k += 1
                    residual(p3, k, base)
                    normalise(1, p3)
                if last:
                    dve.wait_ge(in_half[0], 32)
                    for U in range(3):
                        k += chunk0(U, k, base)
                if not first:
                    split_lo(1, p3, p3 * C)
                for c in range(GC):
                    if last and c < 3:
                        k += chunk0(3 + c, k, base)
                    v_out(g, c)
                if first:
                    for kk in range(KT):
                        dve.wait_ge(wo_hi, kk + 1)
                        V.tensor_tensor(wo_hl[:, 1, kk, :], wo_in[:, kk, :], wo_hl[:, 0, kk, :],
                                        ALU.subtract).then_inc(wo_lo, 1)
                    dve.wait_ge(in_x, 16 * (G - 1))
                for c in range(GC):
                    k += slot(g * GC + c, c, base + k, last)
                return k

            links[0] += group(0, links[0], first=True)
            base = links[0]
            per = 1 + GC + (GC - 1)
            with dve.Fori(1, G - 1) as g:
                assert group(g, (g - 1) * per + base) == per
            links[0] = base + (G - 2) * per
            links[0] += group(G - 1, links[0], last=True)
            att_lo(NCH - 1)
            split_lo(1, NCH - 2, (NCH - 2) * C)
            links[0] += 1
            residual(NCH - 1, 0, links[0])
            normalise(1, NCH - 1)
            split_lo(1, NCH - 1, (NCH - 1) * C)

            def accumulate(tile_no, t):
                for q in range(GC):
                    n = t * GC + q
                    dve.wait_ge(dn_mm, tile_no * (FT * GC) + ((FT - 1) * GC + q + 1))
                    V.scalar_tensor_tensor(xs[:, n * D:(n + 1) * D], B[4 + q][:, :], 1.0 / (W_SCALE * MLP_SCALE),
                                           xs[:, n * D:(n + 1) * D], ALU.mult, ALU.add).then_inc(acc_done, 1)

            def chunk(c, par, base, first=False, last=False):
                k = 0
                for t in range(NT):
                    for ft in range(FT):
                        s = c * STEPS + (t * FT + ft)
                        b = ft % 2
                        unit = ft > 0 and not last
                        th, nib, m = t // 2, t % 2, ft - 1
                        i = 3 * t + m
                        dve.wait_ge(sq_done, s + 1)
                        V.scalar_tensor_tensor(T[b], T[b], 1.0 / GELU_B, B[b][:, :], ALU.add, ALU.mult).then_inc(u_done, 1)
                        if unit:
                            if ft == 1 and t % 2 == 0:
                                dve.wait_ge(in_half[th], (c + 2) * 32)
                            k += decode(i, th, nib, m, k, base)
                        dve.wait_ge(th_done, s + 1)
                        V.scalar_tensor_tensor(T[b], T[b], 1.0, B[b][:, :], ALU.add, ALU.mult).then_inc(w_done, 1)
                        dve.wait_ge(w_done, s + 1)
                        dve.wait_ge(up_mm, s + 1)
                        V.scalar_tensor_tensor(T[b], T[b], 0.5 * MLP_SCALE / (W_SCALE * W_SCALE), B[2 + b][:, :],
                                               ALU.mult, ALU.mult).then_inc(z_done, 1)
                        dve.wait_ge(zhi_done, s + 1)
                        V.tensor_tensor(zhl[:, b, 1, :], T[b], zhl[:, b, 0, :], ALU.subtract).then_inc(zlo_done, 1)
                        if unit:
                            weight_lo(c * UNITS + (UNITS + i), i, ffw[1 - par][:, th, nib, :, m, :])
                        if ft == 0 and not (first and t == 0):
                            accumulate(c * NT + (t - 1), (t - 1) % NT)
                return k

            links[0] += chunk(0, 0, links[0], first=True)
            base = links[0]
            per = 2 * UNITS
            with dve.Fori(0, (NF - 2) // 2) as cp:
                assert chunk(cp * 2 + 1, 1, cp * (2 * per) + base) == per
                assert chunk(cp * 2 + 2, 0, cp * (2 * per) + (base + per)) == per
            chunk(NF - 1, 1, 0, last=True)
            accumulate(NF * NT - 1, NT - 1)

        @block.tensor
        def _(pe):
            T_ = nc.tensor

            def mod_row_mm(j):
                pe.wait_ge(colsum_done, j + 1)
                if j >= 2:
                    pe.wait_ge(mod_row, j - 1)
                T_.matmul(B[6 + j % 2][:, :], ones[:, :], colsum[j % 2], start=True, stop=True).then_inc(mod_mm, 1)

            def ln_transpose(ln, m, bank_free, bank=None):
                if bank is None:
                    pe.wait_ge(ht_done[ln], count(ln, m))
                for s_, v_ in bank_free:
                    wait(pe, s_, v_)
                for k in range(KT):
                    if ln == 0:
                        src = (ht[0] if bank is None else ht_first[m])[:, k * P:(k + 1) * P]
                    else:
                        src = ht[1][:, :].rearrange("p (j q two) -> p j two q", j=2, two=2)[:, k // 2, k % 2, :]
                    ins = T_.transpose(B[(5, 7)[ln] if bank is None else bank][:, k * P:(k + 1) * P], src, ident[:, :])
                ins.then_inc(lt_done[ln], 1)

            def three(out_, whi, wlo, mhi, mlo, start, stop):
                T_.matmul(out_, whi, mhi, start=start, stop=False)
                T_.matmul(out_, whi, mlo, start=False, stop=False)
                return T_.matmul(out_, wlo, mhi, start=False, stop=stop)

            def qk_tile(g, i):
                b = i % 4
                if i >= 4:
                    pe.wait_ge(qk_done, g * 8 + i - 3)
                j, col = i // KT, i % KT * P
                for k in range(KT):
                    ins = three(B[b][:, :], wqkv_hl[:, j, 0, k, col:col + P], wqkv_hl[:, j, 1, k, col:col + P],
                                h1_hl[:, 0, k, :], h1_hl[:, 1, k, :], k == 0, k == KT - 1)
                ins.then_inc(qk_mm, 1)

            def v_tile(g, c):
                pe.wait_ge(qk_done, g * 8 + 5 + c)
                for k in range(KT):
                    ins = three(B[c][:, :], h1_hl[:, 0, k, c * C:(c + 1) * C], h1_hl[:, 1, k, c * C:(c + 1) * C],
                                wqkv_hl[:, 2, 0, k, :], wqkv_hl[:, 2, 1, k, :], k == 0, k == KT - 1)
                ins.then_inc(v_mm, 1)

            def out_proj(n):
                pe.wait_ge(ahi_done, n + 1)
                pe.wait_ge(alo_done, n + 1)
                pe.wait_ge(kd_done, n + 1)
                for k in range(KT):
                    a = att_hl[:, :, k * P:(k + 1) * P]
                    ins = three(B[4][:, :], a[:, 0, :], a[:, 1, :], wo_hl[:, 0, k, :], wo_hl[:, 1, k, :], k == 0, k == KT - 1)
                ins.then_inc(wo_mm, 1)

            def ln2(m):
                ln_transpose(1, m, [(hhi_done[1], m), (hlo_done[1], m)])

            mod_row_mm(0)
            mod_row_mm(1)
            for m in range(GC):
                pe.wait_ge(*((ht012_done, m + 1) if m < 3 else (ht3_done, 1)))
                ln_transpose(0, m, [], bank=m)

            def slot(g, c, last):
                n = g * GC + c
                if c == 0:
                    pe.wait_ge(qk_done, g * 8 + 8)
                    wait(pe, x1_done, n)
                elif c > 1:
                    pe.wait_ge(x1_done, n - 1)
                else:
                    pe.wait_ge(kd_done, n)
                for k in range(KT):
                    ins = T_.transpose(B[4][:, k * P:(k + 1) * P], kT[:, k, c * C:(c + 1) * C], ident[:, :])
                ins.then_inc(kt_mm, 1)
                for r in range(R):
                    if c == 0:
                        pe.wait_ge(v_done, n + r + 1)
                    rows = slice(HD * r, HD * r + HD)
                    for k in range(KT):
                        ins = T_.matmul(B[r][:, k * C:(k + 1) * C], kT[rows, k, c * C:(c + 1) * C],
                                        qT[rows, k, c * C:(c + 1) * C], start=True, stop=True)
                    ins.then_inc(sc_mm, 1)
                pe.wait_ge(kd_done, n + 1)
                if not last:
                    pe.wait_ge(hhi_done[0], n + GC)
                    pe.wait_ge(hlo_done[0], n + GC)
                elif c > 0:
                    pe.wait_ge(snew_done, n)
                else:
                    pe.wait_ge(hhi_done[0], NCH)
                    pe.wait_ge(hlo_done[0], NCH)
                for k in range(KT):
                    ins = T_.matmul(B[5][:, k * P:(k + 1) * P], kd[:, k * P:(k + 1) * P],
                                    vv[:, c, k * P:(k + 1) * P], start=True, stop=True)
                ins.then_inc(st_mm, 1)
                if c > 0:
                    out_proj(n - 1)
                pe.wait_ge(qd_done, n + 1)
                pe.wait_ge(S_done, n + 1)
                for k in range(KT):
                    T_.matmul(B[6][:, k * P:(k + 1) * P], S[:, c % 2, k * P:(k + 1) * P], qd[:, k * P:(k + 1) * P],
                              start=(k == 0), stop=False, skip_group_check=True)
                for r in range(R):
                    pe.wait_ge(pr_done, R * n + r + 1)
                    for k in range(KT):
                        h0 = (R * k + r) * HD
                        ins = T_.matmul(B[6][HD * r:HD * r + HD, k * P:(k + 1) * P], vv[:, c, h0:h0 + HD],
                                        pr_rg[:, r, k, :], start=False,
                                        stop=(r == R - 1 and k == KT - 1), skip_group_check=True)
                ins.then_inc(av_mm, 1)
                if not last:
                    ln_transpose(0, n + GC, [(snew_done, n + 1)])
                if c > 1:
                    ln2(n - 2)

            def group(g, first=False, last=False):
                pe.wait_ge(hhi_done[0], g * GC + GC)
                pe.wait_ge(hlo_done[0], g * GC + GC)
                for i in range(8):
                    if first and i % KT == 0:
                        pe.wait_ge(wq_lo, (i // KT + 1) * KT)
                    qk_tile(g, i)
                    if first and i > 4:
                        mod_row_mm(i - 3)
                    if not first:
                        if i == 0:
                            ln2(g * GC - 2)
                        if i == 1:
                            out_proj(g * GC - 1)
                        if i == 5:
                            ln2(g * GC - 1)
                if first:
                    pe.wait_ge(wq_lo, 3 * KT)
                for c in range(GC):
                    v_tile(g, c)
                    if first and c == 0:
                        mod_row_mm(5)
                if first:
                    pe.wait_ge(mask_done, R)
                    pe.wait_ge(mod_row, 6)
                    pe.wait_ge(wo_lo, KT)
                for c in range(GC):
                    slot(g, c, last)

            group(0, first=True)
            with pe.Fori(1, G - 1) as g:
                group(g)
            group(G - 1, last=True)

            def gate_up(c, par, t, ft, first_steps):
                s = c * STEPS + t * FT + ft
                for m, (sem_free, sem_out) in enumerate(((w_done, gate_mm), (z_done, up_mm))):
                    if not first_steps:
                        pe.wait_ge(sem_free, s - 1)
                    for k in range(KT):
                        w = ffw[par][:, k // 2, k % 2, :, m, ft * P:(ft + 1) * P]
                        ins = three(B[2 * m + ft % 2][:, :], w[:, 0, :], w[:, 1, :],
                                    h2hi[:, k, bass.ds(t * GT, GT)], h2lo[:, k, bass.ds(t * GT, GT)],
                                    k == 0, k == KT - 1)
                    ins.then_inc(sem_out, 1)

            def down(s, par, tile_no, ft, first_tile=False):
                pe.wait_ge(zhi_done, s + 1)
                pe.wait_ge(zlo_done, s + 1)
                for q in range(GC):
                    if ft == 0 and not first_tile:
                        pe.wait_ge(acc_done, tile_no * GC + (q + 1 - GC))
                    z = zhl[:, ft % 2, :, q * P:(q + 1) * P]
                    w = ffw[par][:, ft // 2, ft % 2, :, 2, :]
                    ins = three(B[4 + q][:, :], z[:, 0, :], z[:, 1, :], w[:, 0, :], w[:, 1, :], ft == 0, ft == FT - 1)
                    ins.then_inc(dn_mm, 1)

            def weights_ready(c):
                pe.wait_ge(whi_done, c * UNITS + UNITS)
                pe.wait_ge(wlo_done, c * UNITS + UNITS)

            def chunk(c, par, first=False):
                weights_ready(c)
                s0 = c * STEPS
                for ft in range(FT):
                    if first and ft == 0:
                        pe.wait_ge(hhi_done[1], GC)
                        pe.wait_ge(hlo_done[1], GC)
                    gate_up(c, par, 0, ft, first and ft < 2)
                    if first and ft == 0:
                        ln2(NCH - 2)
                        out_proj(NCH - 1)
                    elif first and ft == 1:
                        ln2(NCH - 1)
                        pe.wait_ge(hhi_done[1], NCH)
                        pe.wait_ge(hlo_done[1], NCH)
                        down(s0, par, 0, 0, first_tile=True)
                    elif ft == 0:
                        down(s0 - 1, 1 - par, c * NT - 1, FT - 1)
                    else:
                        down(s0 + ft - 1, par, c * NT, ft - 1)
                with pe.Fori(1, NT) as t:
                    for ft in range(FT):
                        gate_up(c, par, t, ft, False)
                        s = s0 + t * FT + ft
                        if ft == 0:
                            down(s - 1, par, c * NT + t - 1, FT - 1)
                        else:
                            down(s - 1, par, c * NT + t, ft - 1)

            chunk(0, 0, first=True)
            with pe.Fori(0, (NF - 2) // 2) as cp:
                chunk(cp * 2 + 1, 1)
                chunk(cp * 2 + 2, 0)
            chunk(NF - 1, 1)
            down(NF * STEPS - 1, 1, NF * NT - 1, FT - 1)


def kernel(**inputs):
    import numpy as np
    import concourse.bacc as bacc
    from concourse.bass_utils import run_bass_kernel_spmd

    a = {name: np.asarray(v) for name, v in inputs.items()}

    def up_codes(w):
        w = w.reshape(NF, 2, P, 2, 2, P)
        return w.transpose(0, 4, 5, 1, 3, 2).reshape(NF, 2, P, FC)

    def up_scales(s):
        s = s.reshape(NF, 2, P, 2, 2, 8)
        return s.transpose(0, 4, 5, 1, 3, 2).reshape(NF, 2, 8, FC)

    codes = np.stack([up_codes(a["L0_ffn_gate_W_packed"]), up_codes(a["L0_ffn_up_W_packed"]),
                      a["L0_ffn_down_W_packed"].reshape(D, NF, 2, P).transpose(1, 2, 3, 0)], axis=3)
    scales = np.stack([up_scales(a["L0_ffn_gate_scales"]), up_scales(a["L0_ffn_up_scales"]),
                       a["L0_ffn_down_scales"].reshape(D, NF, 2, 8).transpose(1, 2, 3, 0)], axis=3)
    arrays = {
        "x": a["L0_attn_x"].reshape(N, D), "wmod": a["L0_wmod"], "cond": a["L0_c"].reshape(KT, P).T,
        "wqkv": a["L0_attn_Wqkv"], "bqkv": a["L0_attn_bqkv"],
        "bqk_cols": a["L0_attn_bqkv"][0:2 * D].reshape(2 * KT, P).T, "wout": a["L0_attn_Wout"],
        "bout": a["L0_attn_bout"], "slopes": a["L0_attn_slopes"],
        "slopes_rg": a["L0_attn_slopes"].reshape(KT, R).T, "codes": codes, "scales": scales,
    }
    arrays = {name: np.ascontiguousarray(v) for name, v in arrays.items()}
    nc = bacc.Bacc("TRN2", target_bir_lowering=False, num_devices=1)
    aps = {name: nc.dram_tensor(name, v.shape, mybir.dt.from_np(v.dtype), kind="ExternalInput").ap()
           for name, v in arrays.items()}
    out = nc.dram_tensor("out", (N, D), F32, kind="ExternalOutput").ap()
    adaln_block_kernel(nc, out=out, **aps)
    r = run_bass_kernel_spmd(nc, [arrays], core_ids=[0])
    return r.results[0]["out"].reshape(1, N, D)
```

```python
from contextlib import ExitStack

import concourse.bass as bass
from concourse import mybir

F32 = mybir.dt.float32
F16 = mybir.dt.float16
I32 = mybir.dt.int32
ALU = mybir.AluOpType
ACT = mybir.ActivationFunctionType

P = 128
N = 2048
D = 512
KT = D // P
H = 16
HD = D // H
R = P // HD
C = P
NCH = N // C
GC = 4
G = NCH // GC
GT = GC * C
F = 4096
FC = 512
NF = F // FC
FT = FC // P
NT = N // GT
STEPS = NT * FT
UNITS = 12
EPS = 1e-5

W_SCALE = 2.0 ** 8
ATT_SCALE = 2.0 ** -4
MLP_SCALE = 2.0 ** -3
CODE_SCALE = 2.0 ** 14
CODE_MASK = 0x8E000000 - (1 << 32)
GELU_A = 0.7978845608028654
GELU_B = 0.044715


def adaln_block_kernel(nc, x, wmod, cond, wqkv, bqkv, bqk_cols, wout, bout, slopes, slopes_rg, codes, scales, out):
    with ExitStack() as ctx:
        def sb(name, shape, dt=F32):
            return ctx.enter_context(nc.sbuf_tensor(name, shape, dt))

        def sem(name):
            return ctx.enter_context(nc.semaphore(name))

        xs = sb("xs", [P, NCH * D])
        h2 = sb("h2", [P, 2 * KT * N], F16)
        h2hi = h2[:, 0:KT * N].rearrange("p (k t) -> p k t", k=KT)
        h2lo = h2[:, KT * N:2 * KT * N].rearrange("p (k t) -> p k t", k=KT)
        h2_f32 = h2[:, :].bitcast(F32)
        wq_in = [h2_f32[:, j * 2048:(j + 1) * 2048].rearrange("p (k n) -> p k n", k=KT) for j in range(3)]
        wo_in = h2_f32[:, 6144:8192].rearrange("p (k n) -> p k n", k=KT)

        wa = sb("wa", [P, 2 * KT * 3 * D], F16)
        wqkv_hl = wa[:, :].rearrange("p (j s k n) -> p j s k n", j=3, s=2, k=KT)
        qkv = sb("qkv", [P, 3 * KT * GT])
        qT, kT = (qkv[:, j * 2048:(j + 1) * 2048].bitcast(F16).rearrange("p (s g t) -> p s g t", s=2, g=KT)
                  for j in range(2))
        vv = qkv[:, 4096:6144].rearrange("p (c n) -> p c n", c=GC)
        wb = qkv[:, :].bitcast(F16)
        ffw = [w.rearrange("p (t b s m n) -> p t b s m n", t=2, b=2, s=2, m=3) for w in (wa[:, :], wb)]

        wo = sb("wo", [P, 2 * KT * D], F16)
        wo_hl = wo[:, :].rearrange("p (s k n) -> p s k n", s=2, k=KT)
        h1 = sb("h1", [P, 2 * KT * GT], F16)
        h1_hl = h1[:, :].rearrange("p (s k t) -> p s k t", s=2, k=KT)

        stage = sb("stage", [P, 4608])
        wm_in = [stage[:, j * 2048:(j + 1) * 2048].rearrange("p (k n) -> p k n", k=KT) for j in range(2)]
        pk = stage[:, 0:3072].bitcast(I32).rearrange("p (t m n) -> p t m n", t=2, m=3)
        scl = [stage[:, 3072:4608].rearrange("p (m n) -> p m n", m=3),
               h1[:, 0:3072].bitcast(F32).rearrange("p (m n) -> p m n", m=3)]

        wf = sb("wf", [P, 2, D])
        mask = sb("mask", [P, R * KT * C])
        mask_r = mask[:, :].rearrange("p (r n) -> p r n", r=R)
        pr = sb("pr", [P, R * KT * C])
        pr_r = pr[:, :].rearrange("p (r n) -> p r n", r=R)
        pr_rg = pr[:, :].rearrange("p (r g i) -> p r g i", r=R, g=KT)
        qk_f = [pr[:, j * D:(j + 1) * D] for j in range(2)]
        colsum = [wf[:, j, :] for j in range(2)]
        gt = [pr[:, 2 * D:3 * D], pr[:, 3 * D:4 * D]]
        T = [mask[:, j * D:(j + 1) * D] for j in range(2)]
        zhl = pr[:, 0:2 * D].bitcast(F16).rearrange("p (b s n) -> p b s n", b=2, s=2)

        qdec = sb("qdec", [P, KT * C])
        kdec = sb("kdec", [P, H])
        sdec, Sc, Sd, kv = (sb(n, [P, KT * HD]) for n in ("sdec", "Sc", "Sd", "kv"))
        kd = sb("kd", [P, D])
        qd = sb("qd", [P, KT * C])
        S = sb("S", [P, 2, D])
        ga_bc = sb("ga_bc", [P, D])
        att_hl = sb("att_hl", [P, 2, D], F16)
        ht1 = [sb(f"ht1_{c}", [P, D])[:, :] for c in range(GC)]
        ht2 = [sb(f"ht2_{odd}", [P, D])[:, :] for odd in range(2)]
        ht = [ht1, ht2]
        xint = sb("xint", [P, D], I32)
        gb_bc = sb("gb_bc", [P, D])
        bga = sb("bga", [P, D])
        bv_bc = sb("bv_bc", [P, D])
        ident = sb("ident", [P, P])
        ident16 = sb("ident16", [P, P], F16)
        ones = sb("ones", [P, P])
        dif = kd[:, 0:P].bitcast(I32)
        difc = gt[0][:, 0:P]
        ge = gt[0][:, P:2 * P]
        idx = gt[0][:, 2 * P:3 * P]
        small = sb("small", [P, 144])
        cT, ce, c1, sil = (small[:, 4 * j:4 * j + 4] for j in range(4))
        spart = small[:, 16:20]
        nsp = small[:, 20:24]
        bdec = small[:, 24:28]
        bqk = small[:, 28:36]
        nsl = small[:, 36:52]
        cj = small[:, 52:53]
        epow4 = small[:, 96:100]
        epow = epow4[:, 0:1]
        epsc4 = small[:, 100:104]
        epsc = epsc4[:, 0:1]
        mv4 = small[:, 104:112]
        stat4 = small[:, 120:144]
        ve4, rs4 = small[:, 112:116], small[:, 116:120]
        stat = small[:, 54:60]
        mv = small[:, 60:62]
        ve = small[:, 62:63]
        rs = small[:, 63:64]
        slp = small[:, 76:92]
        tick, tick_x = small[:, 92:93], small[:, 93:94]
        ints = sb("ints", [P, 1], I32)
        mcol = sb("mcol", [P, 2, 2, KT])
        idxi = xint[:, 0:P]

        B = [ctx.enter_context(nc.psum_tensor(f"bank{b}", [P, 512], F32)) for b in range(8)]

        in_small, in_wmod0, in_wmod1, in_x0, in_x1, in_x, in_wout = (
            sem(n) for n in ("in_small", "in_wmod0", "in_wmod1", "in_x0", "in_x1", "in_x", "in_wout"))
        in_cond, in_rows = sem("in_cond"), sem("in_rows")
        in_wmod = [in_wmod0, in_wmod1]
        in_wq = [sem(f"in_wq{j}") for j in range(3)]
        in_half = [sem("in_half0"), sem("in_half1")]
        out_done = sem("out_done")
        iota_done, const_done, exp_done, mask_done, sdec_done = (
            sem(n) for n in ("iota_done", "const_done", "exp_done", "mask_done", "sdec_done"))
        silu_exp, silu_done, colsum_done, mod_mm, mod_row, gates_done = (
            sem(n) for n in ("silu_exp", "silu_done", "colsum_done", "mod_mm", "mod_row", "gates_done"))
        col_mm, col_done = sem("col_mm"), sem("col_done")
        wq_hi, wq_lo, wo_f, wo_hi, wo_lo = (sem(n) for n in ("wq_hi", "wq_lo", "wo_f", "wo_hi", "wo_lo"))
        dve_chain, pool_chain = sem("dve_chain"), sem("pool_chain")
        stats4_done, rstd4_done, norm1_done = (sem(n) for n in ("stats4_done", "rstd4_done", "norm1_done"))
        stats2_done, rstd2_done, norm2_done = (sem(n) for n in ("stats2_done", "rstd2_done", "norm2_done"))
        lt_done = [sem("lt1_done"), sem("lt2_done")]
        hm_done = [sem("hm1_done"), sem("hm2_done")]
        hhi_done = [sem("h1hi_done"), sem("h2hi_done")]
        hlo_done = [sem("h1lo_done"), sem("h2lo_done")]
        xb_done, x1_done = sem("xb_done"), sem("x1_done")
        qk_mm, qk_done, v_mm, v_done = (sem(n) for n in ("qk_mm", "qk_done", "v_mm", "v_done"))
        qk_hi, qk_lo = sem("qk_hi"), sem("qk_lo")
        kt_mm, kd_done, sc_mm, pr_done = (sem(n) for n in ("kt_mm", "kd_done", "sc_mm", "pr_done"))
        kv_mm, kv_done, Sc_done, S_done, qd_done = (sem(n) for n in ("kv_mm", "kv_done", "Sc_done", "S_done", "qd_done"))
        av_mm, ahi_done, alo_done, wo_mm = (sem(n) for n in ("av_mm", "ahi_done", "alo_done", "wo_mm"))
        wf_done, whi_done, wlo_done = (sem(n) for n in ("wf_done", "whi_done", "wlo_done"))
        gate_mm, up_mm, dn_mm = (sem(n) for n in ("gate_mm", "up_mm", "dn_mm"))
        sq_done, u_done, th_done, w_done, z_done, zhi_done, zlo_done, acc_done = (
            sem(n) for n in ("sq_done", "u_done", "th_done", "w_done", "z_done", "zhi_done", "zlo_done", "acc_done"))

        block = ctx.enter_context(nc.Block())

        def wait(eng, s_, v_):
            if not (isinstance(v_, int) and v_ <= 0):
                eng.wait_ge(s_, v_)

        def xrow(n):
            return xs[:, bass.ds(n * D, D)]

        MODS = ["sa", "ca", "ga", "sb", "cb", "gb"]
        PIECES = ["sa", "ca", "ga", "gb", "sb", "cb"]

        def chunk0_unit(U):
            return ffw[0][:, U // 6, U // 3 % 2, :, U % 3, :]

        def chunk0_slot(c):
            return ((6,), (7, 8), (9, 10), (11,))[c]

        @block.sync
        def _(sp):
            sp.dma_start(cT, cond).then_inc(in_cond, 16)
            wm = wmod.rearrange("(k p) (s n) -> p k s n", p=P, s=6)

            def load_wmod(j):
                if j > 1:
                    sp.wait_ge(colsum_done, j - 1)
                sp.dma_start(wm_in[j % 2], wm[:, :, MODS.index(PIECES[j]), :]).then_inc(in_wmod[j % 2], 16)

            xv = x.rearrange("(g c p) n -> g p c n", p=P, c=GC)
            wqv = wqkv.rearrange("(k p) (j n) -> j p k n", p=P, j=3)

            def load_x(g, landed):
                sp.dma_start(xs[:, g * GC * D:(g + 1) * GC * D].rearrange("p (c n) -> p c n", c=GC),
                             xv[g]).then_inc(landed, 16)

            def load_wq(j):
                sp.dma_start(wq_in[j], wqv[j]).then_inc(in_wq[j], 16)

            load_x(0, in_x0)
            load_wmod(0)
            load_wmod(1)
            load_wq(0)
            for r in range(R):
                sp.dma_start(spart[HD * r:HD * r + HD, :],
                             slopes_rg[r:r + 1, :].to_broadcast([HD, KT])).then_inc(in_small, 16)
            row = slopes.rearrange("(a n) -> a n", a=1)
            sp.dma_start(slp, row.to_broadcast([P, H])).then_inc(in_small, 16)
            sp.dma_start(bqk, bqk_cols).then_inc(in_small, 16)
            load_wq(1)
            brow = bqkv.rearrange("(a n) -> a n", a=1)
            sp.dma_start(bv_bc[:, :], brow[:, 2 * D:3 * D].to_broadcast([P, D])).then_inc(in_rows, 16)
            sp.dma_start(bga[:, :], bout.rearrange("(a n) -> a n", a=1).to_broadcast([P, D])).then_inc(in_rows, 16)
            load_wq(2)
            load_wmod(2)
            load_wmod(3)
            sp.dma_start(wo_in, wout.rearrange("(k p) n -> p k n", p=P)).then_inc(in_wout, 16)
            load_x(1, in_x1)
            load_wmod(4)
            load_wmod(5)
            for g in range(2, G):
                load_x(g, in_x)

            def load_half(c, t):
                sp.dma_start(pk[:, t, :, :], codes[bass.ds(c, 1), t].rearrange("a p m n -> (a p) m n")).then_inc(in_half[t], 16)
                src = scales[bass.ds(c, 1), t].rearrange("a b m n -> (a b) (m n)").unsqueeze(1)
                sp.dma_start(scl[t].rearrange("p m n -> p (m n)"),
                             src.to_broadcast([8, 16, 3 * D])).then_inc(in_half[t], 16)

            sp.wait_ge(colsum_done, 6)
            load_half(0, 0)
            sp.wait_ge(v_mm, NCH)
            load_half(0, 1)
            with sp.Fori(1, NF) as c:
                for t in range(2):
                    sp.wait_ge(wf_done, c * UNITS - UNITS + 6 * (t + 1))
                    load_half(c, t)
            ov = out.rearrange("(n p) d -> n p d", p=P)
            for n in range(NCH):
                sp.wait_ge(acc_done, NCH * (NF - 1) + n + 1)
                sp.dma_start(ov[n], xs[:, n * D:(n + 1) * D]).then_inc(out_done, 16)
            sp.wait_ge(out_done, 16 * NCH)

        @block.gpsimd
        def _(pool):
            nc.gpsimd.iota(dif, pattern=[[1, P]], base=0, channel_multiplier=-1).then_inc(iota_done, 1)
            nc.gpsimd.iota(idxi, pattern=[[1, P]], base=0, channel_multiplier=0).then_inc(iota_done, 1)
            nc.gpsimd.iota(ints[:, :], pattern=[[1, 1]], base=C, channel_multiplier=-1).then_inc(iota_done, 1)
            nc.gpsimd.memset(epow4, -0.5)
            nc.gpsimd.memset(epsc4, EPS).then_inc(pool_chain, 1)
            chain = [1]

            def ln1_rstd(g, base):
                pool.wait_ge(stats4_done, g + 1)
                nc.gpsimd.tensor_tensor(ve4, mv4.rearrange("p (c two) -> p two c", two=2)[:, 1, :], epsc4,
                                        ALU.add).then_inc(pool_chain, 1)
                pool.wait_ge(pool_chain, base + 1)
                nc.gpsimd.tensor_tensor(rs4, ve4, epow4, ALU.pow).then_inc(rstd4_done, 1)

            def ln2_rstd(n, base):
                pool.wait_ge(stats2_done, n + 1)
                nc.gpsimd.tensor_tensor(ve, mv[:, 1:2], epsc, ALU.add).then_inc(pool_chain, 1)
                pool.wait_ge(pool_chain, base + 1)
                nc.gpsimd.tensor_tensor(rs, ve, epow, ALU.pow).then_inc(rstd2_done, 1)

            def add_bias(m):
                nc.gpsimd.tensor_tensor(xrow(m), xrow(m), bga[:, :], ALU.add).then_inc(xb_done, 1)

            def weight_lo(tiles):
                for U in tiles:
                    pool.wait_ge(whi_done, U + 1)
                    dst = chunk0_unit(U)
                    nc.gpsimd.tensor_tensor(dst[:, 1], wf[:, U % 2, :], dst[:, 0], ALU.subtract).then_inc(wlo_done, 1)

            def decayed_q(n, c, base):
                wait(pool, av_mm, n)
                hi, lo = (qT[:, j, :, c * C:(c + 1) * C] for j in range(2))
                nc.gpsimd.tensor_tensor(qd[:, :].rearrange("p (g i) -> p g i", g=KT), hi, lo,
                                        ALU.add).then_inc(pool_chain, 1)
                pool.wait_ge(pool_chain, base + 1)
                nc.gpsimd.tensor_tensor(qd[:, :], qd[:, :], qdec[:, :], ALU.mult).then_inc(qd_done, 1)

            def state(n, base):
                wait(pool, Sc_done, n)
                nc.gpsimd.tensor_tensor(Sd[:, :], Sc[:, :], sdec[:, :], ALU.mult).then_inc(pool_chain, 1)
                pool.wait_ge(pool_chain, base + 1)
                pool.wait_ge(kv_done, n + 1)
                pool.wait_ge(S_done, n + 1)
                nc.gpsimd.tensor_tensor(Sc[:, :], Sd[:, :], kv[:, :], ALU.add).then_inc(Sc_done, 1)

            def group(g, base, first=False, last=False):
                k = 0
                if not first:
                    ln2_rstd(g * GC - 1, base)
                    k += 1
                if last:
                    weight_lo(range(4))
                else:
                    ln1_rstd(g + 1, base + k)
                    k += 1
                pool.wait_ge(qk_lo, g * 8 + 4)
                for c in range(GC):
                    if last and c == 1:
                        weight_lo((6,))
                    decayed_q(g * GC + c, c, base + k)
                    k += 1
                    if last:
                        weight_lo(((4, 5), (7,), (9,), ())[c])
                    if not (last and c == GC - 1):
                        state(g * GC + c, base + k)
                        k += 1
                    if c > 0:
                        ln2_rstd(g * GC + c - 1, base + k)
                        k += 1
                    if last:
                        weight_lo(((), (8,), (10,), (11,))[c])
                    if not last:
                        pool.wait_ge(norm1_done, (g * GC + GC) + (c + 1))
                        add_bias((g + 1) * GC + c)
                return k

            pool.wait_ge(pool_chain, 1)
            ln1_rstd(0, chain[0])
            chain[0] += 1
            pool.wait_ge(gates_done, 2)
            for m in range(GC):
                add_bias(m)
            pool.wait_ge(exp_done, 6)
            pool.wait_ge(sdec_done, 1)
            for k in range(KT):
                pool.wait_ge(wo_hi, k + 1)
                nc.gpsimd.tensor_tensor(wo_hl[:, 1, k, :], wo_in[:, k, :], wo_hl[:, 0, k, :],
                                        ALU.subtract).then_inc(wo_lo, 1)
            chain[0] += group(0, chain[0], first=True)
            per = 1 + 3 * GC
            base = chain[0]
            with pool.Fori(1, G - 1) as g:
                assert group(g, (g - 1) * per + base) == per
            base += (G - 2) * per
            base += group(G - 1, base, last=True)
            ln2_rstd(NCH - 1, base)

        @block.scalar
        def _(act):
            act.wait_ge(in_cond, 16)
            nc.scalar.activation(ce, cT, ACT.Exp, scale=-1.0).then_inc(silu_exp, 1)

            def mod_rows(j):
                act.wait_ge(mod_mm, j + 1)
                nc.scalar.copy((ga_bc, gb_bc)[j][:, :], B[6 + j][:, :]).then_inc(mod_row, 1)

            def modulate(ln, m, i, col):
                act.wait_ge(lt_done[ln], m + 1)
                h = ht[ln][i]
                for k in range(KT):
                    cols = slice(k * C, (k + 1) * C)
                    ins = nc.scalar.activation(h[:, cols], B[(5, 7)[ln]][:, cols], ACT.Identity,
                                               bias=mcol[:, ln, 0, k:k + 1], scale=mcol[:, ln, 1, k:k + 1])
                ins.then_inc(hm_done[ln], 1)
                act.wait_ge(hm_done[ln], m + 1)
                dstT = h1_hl[:, 0, :, col:col + C] if ln == 0 else h2hi[:, :, bass.ds(col, C)]
                nc.scalar.copy(dstT, h.rearrange("p (k t) -> p k t", k=KT)).then_inc(hhi_done[ln], 1)

            def wqkv_hi(j):
                act.wait_ge(in_wq[j], 16)
                for k in range(KT):
                    nc.scalar.activation(wqkv_hl[:, j, 0, k, :], wq_in[j][:, k, :], ACT.Copy,
                                         scale=W_SCALE).then_inc(wq_hi, 1)

            def mask_exp(r):
                for g in range(KT):
                    h = R * g + r
                    nc.scalar.activation(mask_r[:, r, g * C:(g + 1) * C], difc, ACT.Exp,
                                         scale=nsl[:, h:h + 1]).then_inc(exp_done, 1)

            wqkv_hi(0)
            act.wait_ge(col_done, 1)
            for k in range(KT):
                act.wait_ge(lt_done[0], k + 1)
                nc.scalar.activation(ht1[k], B[k][:, :], ACT.Identity, bias=mcol[:, 0, 0, k:k + 1],
                                     scale=mcol[:, 0, 1, k:k + 1]).then_inc(hm_done[0], 1)
                act.wait_ge(hm_done[0], k + 1)
                nc.scalar.copy(h1_hl[:, 0, k, :], ht1[k]).then_inc(hhi_done[0], 1)
            wqkv_hi(1)
            act.wait_ge(const_done, 1)

            def beside_qk(i):
                if i == 0:
                    wqkv_hi(2)
                elif i == 1:
                    nc.scalar.activation(bdec, nsp, ACT.Exp, scale=float(C)).then_inc(exp_done, 1)
                    nc.scalar.activation(kdec[:, :], nsl, ACT.Exp, scale=cj).then_inc(exp_done, 1)
                    for g in range(KT):
                        nc.scalar.activation(qdec[:, g * C:(g + 1) * C], idx, ACT.Exp, scale=nsp[:, g:g + 1]).then_inc(exp_done, 1)
                    mask_exp(0)
                elif i == 2:
                    mask_exp(1)
                    mask_exp(2)
                elif i == 3:
                    mask_exp(3)
                elif i == 5 or i == 6:
                    mod_rows(i - 5)

            def att_hi(n):
                act.wait_ge(av_mm, n + 1)
                nc.scalar.activation(att_hl[:, 0, :], B[6][:, :], ACT.Copy, scale=ATT_SCALE).then_inc(ahi_done, 1)

            def qk_out(g, i):
                act.wait_ge(qk_mm, g * 8 + i + 1)
                if not (isinstance(g, int) and g == 0 and i < 2):
                    act.wait_ge(qk_lo, g * 8 + i - 1)
                nc.scalar.activation(qk_f[i % 2], B[i % 4][:, :], ACT.Identity, bias=bqk[:, i:i + 1],
                                     scale=1.0 / W_SCALE).then_inc(qk_done, 1)
                act.wait_ge(qk_done, g * 8 + i + 1)
                nc.scalar.copy((qT, kT)[i // KT][:, 0, i % KT, :], qk_f[i % 2]).then_inc(qk_hi, 1)

            def weight_hi(U, dstW):
                act.wait_ge(wf_done, U + 1)
                nc.scalar.copy(dstW[:, 0], wf[:, U % 2, :]).then_inc(whi_done, 1)

            def group(g, first=False, last=False):
                for i in range(8):
                    qk_out(g, i)
                    if first:
                        beside_qk(i)
                    else:
                        if i == 0:
                            modulate(1, g * GC - 2, 0, (g * GC - 2) * C)
                        if i == 5:
                            modulate(1, g * GC - 1, 1, (g * GC - 1) * C)
                    if last and i == 4:
                        act.wait_ge(qk_mm, NCH * 2 - 4)
                        for U in range(3):
                            weight_hi(U, chunk0_unit(U))
                if first:
                    for k in range(KT):
                        act.wait_ge(wo_f, k + 1)
                        nc.scalar.copy(wo_hl[:, 0, k, :], wo_in[:, k, :]).then_inc(wo_hi, 1)
                if last:
                    act.wait_ge(qk_mm, NCH * 2)
                    for U in range(3, 6):
                        weight_hi(U, chunk0_unit(U))
                for c in range(GC):
                    n = g * GC + c
                    units = chunk0_slot(c) if last else ()
                    if last:
                        act.wait_ge(v_mm, NCH)
                    for U in units if c > 0 else ():
                        weight_hi(U, chunk0_unit(U))
                    if not (last and c == GC - 1):
                        act.wait_ge(kv_mm, n + 1)
                        wait(act, Sc_done, n)
                        nc.scalar.copy(kv[:, :], B[5][:, 0:KT * HD]).then_inc(kv_done, 1)
                    att_hi(n)
                    for U in units if c == 0 else ():
                        weight_hi(U, chunk0_unit(U))
                    if not last:
                        modulate(0, n + GC, c, c * C)
                    if not (last and c == GC - 1):
                        act.wait_ge(Sc_done, n + 1)
                        for r in range(R):
                            rows = slice(HD * r, HD * r + HD)
                            block = S[rows, (c + 1) % 2, :].rearrange("p (g r e) -> p r g e", g=KT, r=R)[:, r]
                            ins = nc.scalar.copy(block, Sc[rows, :].rearrange("p (g e) -> p g e", g=KT))
                        ins.then_inc(S_done, 1)
                    if c > 1:
                        if first and c == 2:
                            act.wait_ge(col_done, 2)
                        modulate(1, n - 2, c % 2, (n - 2) * C)

            group(0, first=True)
            with act.Fori(1, G - 1) as g:
                group(g)
            group(G - 1, last=True)

            def chunk(c, par, first=False, last=False):
                for t in range(NT):
                    for ft in range(FT):
                        s = c * STEPS + (t * FT + ft)
                        b = ft % 2
                        act.wait_ge(gate_mm, s + 1)
                        if not (first and t == 0 and ft < 2):
                            act.wait_ge(zlo_done, s - 1)
                        nc.scalar.activation(T[b], B[b][:, :], ACT.Square, scale=1.0 / W_SCALE).then_inc(sq_done, 1)
                        if first and t == 0 and ft == 0:
                            modulate(1, NCH - 2, 0, (NCH - 2) * C)
                        act.wait_ge(u_done, s + 1)
                        nc.scalar.activation(T[b], T[b], ACT.Tanh, scale=GELU_A * GELU_B / W_SCALE).then_inc(th_done, 1)
                        if ft > 0 and not last:
                            th, nib, m = t // 2, t % 2, ft - 1
                            i = 3 * t + m
                            act.wait_ge(wf_done, c * UNITS + (UNITS + i + 1))
                            wait(act, dn_mm, c * (STEPS * GC))
                            nc.scalar.copy(ffw[1 - par][:, th, nib, 0, m, :], wf[:, i % 2, :]).then_inc(whi_done, 1)
                        act.wait_ge(z_done, s + 1)
                        if not (first and t == 0 and ft < 2):
                            act.wait_ge(dn_mm, c * (STEPS * GC) + GC * (t * FT + ft - 1))
                        nc.scalar.copy(zhl[:, b, 0, :], T[b]).then_inc(zhi_done, 1)
                        if first and t == 0 and ft == 0:
                            modulate(1, NCH - 1, 1, (NCH - 1) * C)

            chunk(0, 0, first=True)
            with act.Fori(0, (NF - 2) // 2) as cp:
                chunk(cp * 2 + 1, 1)
                chunk(cp * 2 + 2, 0)
            chunk(NF - 1, 1, last=True)

        @block.vector
        def _(dve):
            links = [0]

            def link(ins, base, k):
                ins.then_inc(dve_chain, 1)
                dve.wait_ge(dve_chain, base + k)

            def link0(ins):
                links[0] += 1
                link(ins, links[0], 0)

            V = nc.vector
            V.memset(ones[:, :], 1.0)
            V.memset(Sc[:, :], 0.0)
            V.memset(S[:, :, :], 0.0).then_inc(S_done, 1)
            dve.wait_ge(iota_done, 3)
            V.tensor_scalar(ident[:, :], dif, 0.0, None, ALU.is_equal)
            V.tensor_scalar(ident16[:, :], dif, 0.0, None, ALU.is_equal)
            V.tensor_scalar(difc, dif, 0.0, None, ALU.max)
            V.tensor_scalar(ge, dif, 0.0, None, ALU.is_ge)
            V.tensor_copy(idx, idxi)
            V.tensor_copy(cj, ints[:, :])
            dve.wait_ge(in_cond, 16)
            dve.wait_ge(silu_exp, 1)
            link0(V.tensor_scalar(c1, ce, 1.0, None, ALU.add))
            link0(V.reciprocal(ce, c1))
            V.tensor_tensor(sil, cT, ce, ALU.mult).then_inc(silu_done, 1)

            def mod_sum(j, base):
                dve.wait_ge(in_wmod[j % 2], 16 * (j // 2 + 1))
                if j > 1:
                    dve.wait_ge(*((col_mm, j - 1) if j < 4 else (mod_mm, j - 3)))
                w, t = wm_in[j % 2], colsum[j % 2]
                link(V.tensor_scalar(t, w[:, 0, :], sil[:, 0:1], None, ALU.mult), base, 1)
                for k in range(1, KT):
                    ins = V.scalar_tensor_tensor(t, w[:, k, :], sil[:, k:k + 1], t, ALU.mult, ALU.add)
                    if k < KT - 1:
                        link(ins, base, k + 1)
                ins.then_inc(colsum_done, 1)
                return KT - 1

            def columns(ln):
                dve.wait_ge(col_mm, 2 * ln + 2)
                bank = B[(5, 7)[ln]]
                V.tensor_copy(mcol[:, ln, 0, :], bank[:, 0:KT])
                V.tensor_scalar(mcol[:, ln, 1, :], bank[:, KT:2 * KT], 1.0, None, ALU.add).then_inc(col_done, 1)

            def ln1(g, base, k):
                for c in range(GC):
                    ins = V.bn_stats(stat4[:, 6 * c:6 * c + 6], xrow(g * GC + c))
                ins.then_inc(dve_chain, 1)
                dve.wait_ge(dve_chain, base + k)
                V.memset(tick, 0.0)
                for c in range(GC):
                    ins = V.bn_aggr(mv4[:, 2 * c:2 * c + 2], stat4[:, 6 * c:6 * c + 6])
                ins.then_inc(stats4_done, 1)

            def ln1_normalise(g, c):
                return V.tensor_scalar(ht1[c], xrow(g * GC + c), mv4[:, 2 * c:2 * c + 1], rs4[:, c:c + 1],
                                       ALU.subtract, ALU.mult)

            def ln2_normalise(n, odd):
                dve.wait_ge(rstd2_done, n + 1)
                V.tensor_scalar(ht2[odd], xrow(n), mv[:, 0:1], rs, ALU.subtract, ALU.mult).then_inc(norm2_done, 1)

            def split_lo(ln, m, i, col):
                dve.wait_ge(hhi_done[ln], m + 1)
                hi, lo = ((h1_hl[:, j, :, col:col + C] for j in range(2)) if ln == 0 else
                          (h[:, :, bass.ds(col, C)] for h in (h2hi, h2lo)))
                V.tensor_tensor(lo, ht[ln][i].rearrange("p (k t) -> p k t", k=KT), hi,
                                ALU.subtract).then_inc(hlo_done[ln], 1)

            def wq_split(j, tiles=range(KT)):
                for k in tiles:
                    dve.wait_ge(wq_hi, j * KT + k + 1)
                    V.scalar_tensor_tensor(wqkv_hl[:, j, 1, k, :], wq_in[j][:, k, :], W_SCALE,
                                           wqkv_hl[:, j, 0, k, :], ALU.mult, ALU.subtract).then_inc(wq_lo, 1)

            def split_qk(g, i):
                dve.wait_ge(qk_hi, g * 8 + i + 1)
                dstT = (qT, kT)[i // KT]
                V.tensor_tensor(dstT[:, 1, i % KT, :], qk_f[i % 2], dstT[:, 0, i % KT, :], ALU.subtract).then_inc(qk_lo, 1)

            dve.wait_ge(in_x0, 16)
            links[0] += 1
            ln1(0, links[0], 0)
            dve.wait_ge(silu_done, 1)
            links[0] += mod_sum(0, links[0])
            dve.wait_ge(rstd4_done, 1)
            for c in range(GC):
                ln1_normalise(0, c).then_inc(norm1_done, 1)
            links[0] += mod_sum(1, links[0])
            wq_split(0, range(2))
            columns(0)
            wq_split(0, range(2, KT))
            for k in range(KT):
                dve.wait_ge(hhi_done[0], k + 1)
                V.tensor_tensor(h1_hl[:, 1, k, :], ht1[k], h1_hl[:, 0, k, :], ALU.subtract).then_inc(hlo_done[0], 1)
            dve.wait_ge(in_small, 16 * 6)
            V.tensor_scalar(nsp, spart, -1.0, None, ALU.mult)
            V.tensor_scalar(nsl, slp, -1.0, None, ALU.mult).then_inc(const_done, 1)
            wq_split(1)
            wq_split(2)
            split_qk(0, 0)
            links[0] += mod_sum(2, links[0])
            split_qk(0, 1)
            links[0] += mod_sum(3, links[0])
            split_qk(0, 2)
            dve.wait_ge(exp_done, 6 + R * KT)
            for r in range(R):
                m3 = mask_r[:, r, :].rearrange("p (g i) -> p g i", g=KT)
                V.tensor_tensor(m3, m3, ge.unsqueeze(1).to_broadcast([P, KT, C]), ALU.mult).then_inc(mask_done, 1)
            for g in range(KT):
                ins = V.tensor_scalar(sdec[:, g * HD:(g + 1) * HD], ones[:, 0:HD], bdec[:, g:g + 1], None, ALU.mult)
            ins.then_inc(sdec_done, 1)

            def guard(g_bc, sign, size, base):
                V.tensor_scalar(sign, g_bc[:, :], 0.0, 2.0, ALU.is_ge, ALU.mult)
                link(V.scalar_tensor_tensor(size, g_bc[:, :], -1.0, g_bc[:, :], ALU.mult, ALU.max), base, 1)
                link(V.tensor_scalar(size, size, 0.25, None, ALU.max), base, 2)
                V.scalar_tensor_tensor(g_bc[:, :], sign, -1.0, size, ALU.add, ALU.mult).then_inc(gates_done, 1)
                return 2

            split_qk(0, 3)
            split_qk(0, 4)
            dve.wait_ge(mask_done, R)
            dve.wait_ge(in_rows, 32)
            dve.wait_ge(mod_row, 1)
            links[0] += guard(ga_bc, gt[0], gt[1], links[0])
            dve.wait_ge(gates_done, 1)
            V.tensor_tensor(bga[:, :], bga[:, :], ga_bc[:, :], ALU.mult).then_inc(gates_done, 1)
            split_qk(0, 5)
            dve.wait_ge(in_wout, 16)
            for k in range(KT):
                V.scalar_tensor_tensor(wo_in[:, k, :], wo_in[:, k, :], W_SCALE, ga_bc[:, :], ALU.mult,
                                       ALU.mult).then_inc(wo_f, 1)
            split_qk(0, 6)
            split_qk(0, 7)

            def att_lo(n):
                dve.wait_ge(ahi_done, n + 1)
                V.scalar_tensor_tensor(att_hl[:, 1, :], B[6][:, :], ATT_SCALE, att_hl[:, 0, :], ALU.mult,
                                       ALU.subtract).then_inc(alo_done, 1)

            def residual(n, k0, base):
                dve.wait_ge(wo_mm, n + 1)
                dve.wait_ge(xb_done, n + 1)
                V.scalar_tensor_tensor(xrow(n), B[4][:, :], 1.0 / (W_SCALE * ATT_SCALE), xrow(n), ALU.mult,
                                       ALU.add).then_inc(x1_done, 1)
                dve.wait_ge(x1_done, n + 1)
                V.memset(tick, 0.0)
                V.bn_stats(stat, xrow(n)).then_inc(dve_chain, 1)
                dve.wait_ge(dve_chain, base + k0)
                V.memset(tick, 0.0)
                V.bn_aggr(mv, stat).then_inc(stats2_done, 1)

            def v_out(g, c):
                dve.wait_ge(v_mm, g * GC + c + 1)
                V.scalar_tensor_tensor(vv[:, c, :], B[c][:, :], 1.0 / W_SCALE, bv_bc[:, :], ALU.mult,
                                       ALU.add).then_inc(v_done, 1)

            def decode(i, th, nib, m, k, base):
                codes_t = pk[:, th, m, :]
                sc_t = scl[th][:, m, :]
                if m == 2 and nib == 0:
                    V.tensor_tensor(sc_t, sc_t, gb_bc[:, :], ALU.mult)
                link(V.tensor_scalar(xint[:, :], codes_t, 28 - 4 * nib, 3, ALU.logical_shift_left,
                                     ALU.arith_shift_right), base, k + 1)
                link(V.tensor_scalar(xint[:, :], xint[:, :], CODE_MASK, None, ALU.bitwise_and), base, k + 2)
                val = xint[:, :].bitcast(F16).rearrange("p (n two) -> p n two", two=2)[:, :, 1]
                V.scalar_tensor_tensor(wf[:, i % 2, :], val, CODE_SCALE * W_SCALE, sc_t, ALU.mult,
                                       ALU.mult).then_inc(wf_done, 1)
                return 2

            def weight_lo(U, i, dstW):
                dve.wait_ge(whi_done, U + 1)
                V.tensor_tensor(dstW[:, 1], wf[:, i % 2, :], dstW[:, 0], ALU.subtract).then_inc(wlo_done, 1)

            def chunk0(U, k, base):
                wait(dve, wlo_done, U - 1)
                wait(dve, wf_done, U)
                return decode(U, U // 6, U // 3 % 2, U % 3, k, base)

            def decayed_k(n):
                dve.wait_ge(kt_mm, n + 1)
                V.tensor_tensor(kd[:, :].rearrange("p (h d) -> p h d", h=H),
                                B[4][:, :].rearrange("p (h d) -> p h d", h=H),
                                kdec[:, :].unsqueeze(2).to_broadcast([P, H, HD]), ALU.mult).then_inc(kd_done, 1)

            def slot(n, c, base, first, last):
                k = 0
                units = chunk0_slot(c) if last else ()
                if not (first and c == 0) and not (last and c == GC - 1):
                    decayed_k(n)
                if c > 1:
                    ln2_normalise(n - 2, c % 2)
                if c > 0 and not last:
                    split_lo(0, n + (GC - 1), c - 1, (c - 1) * C)
                if first and c in (1, 2):
                    k += mod_sum(c + 3, base + k)
                for U in units if c > 0 else ():
                    k += chunk0(U, k, base)
                for r in range(R):
                    dve.wait_ge(sc_mm, R * n + r + 1)
                    V.tensor_tensor(pr_r[:, r, :], B[r][:, :], mask_r[:, r, :], ALU.mult).then_inc(pr_done, 1)
                if c == GC - 1:
                    split_lo(1, n - 3, (c + 1) % 2, (n - 3) * C)
                if last and c == 0:
                    dve.wait_ge(in_half[1], 32)
                    for U in units:
                        k += chunk0(U, k, base)
                if c > 0:
                    k += 1
                    residual(n - 1, k, base)
                att_lo(n)
                if first and c == 2:
                    columns(1)
                if c == GC - 1:
                    ln2_normalise(n - 1, (c + 1) % 2)
                    if not last:
                        split_lo(0, n + GC, c, c * C)
                    split_lo(1, n - 2, c % 2, (n - 2) * C)
                return k

            def group(g, base, first=False, last=False):
                k = 0
                p3 = g * GC - 1
                if not first:
                    k += 1
                    residual(p3, k, base)
                if not last:
                    dve.wait_ge(*((in_x1, 16) if first else (in_x, 32)))
                    V.memset(tick_x, 0.0)
                    k += 1
                    ln1(g + 1, base, k)
                    if first:
                        for c in range(GC):
                            v_out(g, c)
                        decayed_k(0)
                    else:
                        split_qk(g, 0)
                    dve.wait_ge(rstd4_done, g + 2)
                    for c in range(GC):
                        ln1_normalise(g + 1, c).then_inc(norm1_done, 1)
                else:
                    split_qk(g, 0)
                    dve.wait_ge(mod_row, 2)
                    k += guard(gb_bc, gt[0], gt[1], base + k)
                    dve.wait_ge(in_half[0], 32)
                    k += chunk0(0, k, base)
                if not first:
                    split_qk(g, 1)
                    ln2_normalise(p3, 1)
                    split_lo(1, p3 - 1, 0, (p3 - 1) * C)
                    split_qk(g, 2)
                    if last:
                        k += chunk0(1, k, base)
                    split_qk(g, 3)
                    split_qk(g, 4)
                    if last:
                        k += chunk0(2, k, base)
                    split_qk(g, 5)
                    split_lo(1, p3, 1, p3 * C)
                    split_qk(g, 6)
                    if last:
                        k += chunk0(3, k, base)
                    split_qk(g, 7)
                    for c in range(GC):
                        if last and c < 2:
                            k += chunk0(4 + c, k, base)
                        v_out(g, c)
                for c in range(GC):
                    k += slot(g * GC + c, c, base + k, first, last)
                return k

            links[0] += group(0, links[0], first=True)
            base = links[0]
            per = 1 + GC
            with dve.Fori(1, G - 1) as g:
                assert group(g, (g - 1) * per + base) == per
            links[0] = base + (G - 2) * per
            links[0] += group(G - 1, links[0], last=True)
            split_lo(1, NCH - 2, 0, (NCH - 2) * C)
            links[0] += 1
            residual(NCH - 1, 0, links[0])

            def accumulate(tile_no, t):
                for q in range(GC):
                    n = t * GC + q
                    dve.wait_ge(dn_mm, tile_no * (FT * GC) + ((FT - 1) * GC + q + 1))
                    V.scalar_tensor_tensor(xs[:, n * D:(n + 1) * D], B[4 + q][:, :], 1.0 / (W_SCALE * MLP_SCALE),
                                           xs[:, n * D:(n + 1) * D], ALU.mult, ALU.add).then_inc(acc_done, 1)

            def chunk(c, par, base, first=False, last=False):
                k = 0
                for t in range(NT):
                    for ft in range(FT):
                        s = c * STEPS + (t * FT + ft)
                        b = ft % 2
                        unit = ft > 0 and not last
                        th, nib, m = t // 2, t % 2, ft - 1
                        i = 3 * t + m
                        dve.wait_ge(sq_done, s + 1)
                        V.scalar_tensor_tensor(T[b], T[b], 1.0 / GELU_B, B[b][:, :], ALU.add, ALU.mult).then_inc(u_done, 1)
                        if first and t == 0 and ft == 0:
                            ln2_normalise(NCH - 1, 1)
                        if unit:
                            if first and t == 0 and ft == 1:
                                dve.wait_ge(wlo_done, UNITS)
                            if ft == 1 and t % 2 == 0:
                                dve.wait_ge(in_half[th], (c + 2) * 32)
                            k += decode(i, th, nib, m, k, base)
                        dve.wait_ge(th_done, s + 1)
                        V.scalar_tensor_tensor(T[b], T[b], 1.0, B[b][:, :], ALU.add, ALU.mult).then_inc(w_done, 1)
                        dve.wait_ge(w_done, s + 1)
                        dve.wait_ge(up_mm, s + 1)
                        V.scalar_tensor_tensor(T[b], T[b], 0.5 * MLP_SCALE / (W_SCALE * W_SCALE), B[2 + b][:, :],
                                               ALU.mult, ALU.mult).then_inc(z_done, 1)
                        dve.wait_ge(zhi_done, s + 1)
                        V.tensor_tensor(zhl[:, b, 1, :], T[b], zhl[:, b, 0, :], ALU.subtract).then_inc(zlo_done, 1)
                        if first and t == 0 and ft == 0:
                            split_lo(1, NCH - 1, 1, (NCH - 1) * C)
                        if unit:
                            weight_lo(c * UNITS + (UNITS + i), i, ffw[1 - par][:, th, nib, :, m, :])
                        if ft == 0 and not (first and t == 0):
                            accumulate(c * NT + (t - 1), (t - 1) % NT)
                return k

            links[0] += chunk(0, 0, links[0], first=True)
            base = links[0]
            per = 2 * UNITS
            with dve.Fori(0, (NF - 2) // 2) as cp:
                assert chunk(cp * 2 + 1, 1, cp * (2 * per) + base) == per
                assert chunk(cp * 2 + 2, 0, cp * (2 * per) + (base + per)) == per
            chunk(NF - 1, 1, 0, last=True)
            accumulate(NF * NT - 1, NT - 1)

        @block.tensor
        def _(pe):
            T_ = nc.tensor

            def mod_row_mm(j):
                pe.wait_ge(colsum_done, j + 3)
                T_.matmul(B[6 + j][:, :], ones[:, :], colsum[j], start=True, stop=True).then_inc(mod_mm, 1)

            def mod_columns(j, bank):
                pe.wait_ge(colsum_done, j + 1)
                for k in range(KT):
                    w = colsum[j % 2][:, k * P:(k + 1) * P]
                    if bank == 7:
                        w = colsum[j % 2].rearrange("p (j q two) -> p j two q", j=2, two=2)[:, k // 2, k % 2, :]
                    col = j % 2 * KT + k
                    ins = T_.matmul(B[bank][:, col:col + 1], w, ones[:, 0:1], start=True, stop=True)
                ins.then_inc(col_mm, 1)

            def transpose4(bank, src, landed):
                for k in range(KT):
                    ins = T_.transpose(B[bank][:, k * P:(k + 1) * P], src(k), ident[:, :])
                ins.then_inc(landed, 1)

            def ln1_transpose(c, bank):
                transpose4(bank, lambda k: ht1[c][:, k * P:(k + 1) * P], lt_done[0])

            def three(out_, whi, wlo, mhi, mlo, start, stop):
                T_.matmul(out_, whi, mhi, start=start, stop=False)
                T_.matmul(out_, whi, mlo, start=False, stop=False)
                return T_.matmul(out_, wlo, mhi, start=False, stop=stop)

            def qk_tile(g, i, first):
                b = i % 4
                if i >= 4:
                    pe.wait_ge(qk_done, g * 8 + i - 3)
                j, col = i // KT, i % KT * P
                for k in range(KT):
                    if first and i == 0:
                        pe.wait_ge(hhi_done[0], k + 1)
                        pe.wait_ge(hlo_done[0], k + 1)
                    ins = three(B[b][:, :], wqkv_hl[:, j, 0, k, col:col + P], wqkv_hl[:, j, 1, k, col:col + P],
                                h1_hl[:, 0, k, :], h1_hl[:, 1, k, :], k == 0, k == KT - 1)
                ins.then_inc(qk_mm, 1)

            def v_tile(g, c):
                pe.wait_ge(qk_done, g * 8 + 5 + c)
                for k in range(KT):
                    ins = three(B[c][:, :], h1_hl[:, 0, k, c * C:(c + 1) * C], h1_hl[:, 1, k, c * C:(c + 1) * C],
                                wqkv_hl[:, 2, 0, k, :], wqkv_hl[:, 2, 1, k, :], k == 0, k == KT - 1)
                ins.then_inc(v_mm, 1)

            def out_proj(n, tiles=range(KT)):
                pe.wait_ge(ahi_done, n + 1)
                pe.wait_ge(alo_done, n + 1)
                for k in tiles:
                    a = att_hl[:, :, k * P:(k + 1) * P]
                    ins = three(B[4][:, :], a[:, 0, :], a[:, 1, :], wo_hl[:, 0, k, :], wo_hl[:, 1, k, :], k == 0, k == KT - 1)
                if k == KT - 1:
                    ins.then_inc(wo_mm, 1)

            def ln2(m, odd):
                pe.wait_ge(norm2_done, m + 1)
                wait(pe, hm_done[1], m)
                h = ht2[odd].rearrange("p (j q two) -> p j two q", j=2, two=2)
                transpose4(7, lambda k: h[:, k // 2, k % 2, :], lt_done[1])

            mod_columns(0, 5)
            for c in range(GC):
                pe.wait_ge(norm1_done, c + 1)
                for k in range(KT):
                    ins = T_.transpose(B[k][:, c * C:(c + 1) * C], ht1[c][:, k * P:(k + 1) * P], ident[:, :])
                    if c == GC - 1:
                        ins.then_inc(lt_done[0], 1)
            mod_columns(1, 5)

            def transpose_k(g, c):
                if c == 0:
                    pe.wait_ge(qk_lo, g * 8 + 8)
                    wait(pe, x1_done, g * GC)
                elif c > 1:
                    pe.wait_ge(x1_done, g * GC + (c - 1))
                else:
                    pe.wait_ge(kd_done, g * GC + c)
                for k in range(KT):
                    for j in range(2):
                        ins = T_.matmul(B[4][:, k * P:(k + 1) * P], kT[:, j, k, c * C:(c + 1) * C], ident16[:, :],
                                        start=(j == 0), stop=(j == 1))
                ins.then_inc(kt_mm, 1)

            def scores(n, c, tiles=range(KT)):
                for k in tiles:
                    for r in range(R):
                        if c == 0 and k == 0:
                            pe.wait_ge(v_done, n + r + 1)
                        rows = slice(HD * r, HD * r + HD)
                        kh, kl, qh, ql = (w[rows, j, k, c * C:(c + 1) * C] for w in (kT, qT) for j in range(2))
                        ins = three(B[r][:, k * C:(k + 1) * C], kh, kl, qh, ql, True, True)
                        if k == KT - 1:
                            ins.then_inc(sc_mm, 1)

            def state_update(n, c, last):
                pe.wait_ge(kd_done, n + 1)
                if c > 0 and last:
                    pe.wait_ge(kv_done, n)
                else:
                    pe.wait_ge(hm_done[0], n + GC)
                for k in range(KT):
                    for r in range(R):
                        h0 = (R * k + r) * HD
                        ins = T_.matmul(B[5][HD * r:HD * r + HD, k * HD:(k + 1) * HD], kd[:, h0:h0 + HD],
                                        vv[:, c, h0:h0 + HD], start=True, stop=True)
                ins.then_inc(kv_mm, 1)

            def slot(g, c, first, last):
                n = g * GC + c
                state = not (last and c == GC - 1)
                if state:
                    transpose_k(g, c)
                if first and c == 1:
                    pe.wait_ge(wo_lo, KT)
                if c == 0:
                    scores(n, c)
                else:
                    scores(n, c, range(0, 2))
                    if state:
                        pe.wait_ge(kd_done, n + 1)
                    else:
                        pe.wait_ge(x1_done, n - 1)
                    out_proj(n - 1, range(0, 2))
                    scores(n, c, range(2, KT))
                    out_proj(n - 1, range(2, KT))
                if state:
                    state_update(n, c, last)
                pe.wait_ge(qd_done, n + 1)
                pe.wait_ge(S_done, n + 1)
                for k in range(KT):
                    T_.matmul(B[6][:, k * P:(k + 1) * P], S[:, c % 2, k * P:(k + 1) * P], qd[:, k * P:(k + 1) * P],
                              start=(k == 0), stop=False, skip_group_check=True)
                for r in range(R):
                    pe.wait_ge(pr_done, R * n + r + 1)
                    for k in range(KT):
                        h0 = (R * k + r) * HD
                        ins = T_.matmul(B[6][HD * r:HD * r + HD, k * P:(k + 1) * P], vv[:, c, h0:h0 + HD],
                                        pr_rg[:, r, k, :], start=False,
                                        stop=(r == R - 1 and k == KT - 1), skip_group_check=True)
                ins.then_inc(av_mm, 1)
                if first and c == 2:
                    mod_columns(4, 7)
                    mod_columns(5, 7)
                if not last:
                    pe.wait_ge(norm1_done, n + GC + 1)
                    pe.wait_ge(kv_done, n + 1)
                    ln1_transpose(c, 5)
                if c > 1:
                    if first and c == 2:
                        pe.wait_ge(col_done, 2)
                    ln2(n - 2, c % 2)

            def group(g, first=False, last=False):
                if not first:
                    out_proj(g * GC - 1)
                    pe.wait_ge(hhi_done[0], g * GC + GC)
                    pe.wait_ge(hlo_done[0], g * GC + GC)
                for i in range(8):
                    if first and i % KT == 0:
                        pe.wait_ge(wq_lo, (i // KT + 1) * KT)
                    qk_tile(g, i, first)
                    if first and i in (5, 6):
                        mod_row_mm(i - 5)
                    if not first:
                        if i == 0:
                            ln2(g * GC - 2, 0)
                        if i == 5:
                            ln2(g * GC - 1, 1)
                if first:
                    pe.wait_ge(wq_lo, 3 * KT)
                for c in range(GC):
                    v_tile(g, c)
                if first:
                    pe.wait_ge(mod_row, 2)
                for c in range(GC):
                    slot(g, c, first, last)

            group(0, first=True)
            with pe.Fori(1, G - 1) as g:
                group(g)
            group(G - 1, last=True)

            def gate_up(c, par, t, ft, first_steps):
                s = c * STEPS + t * FT + ft
                for m, (sem_free, sem_out) in enumerate(((w_done, gate_mm), (z_done, up_mm))):
                    if not first_steps:
                        pe.wait_ge(sem_free, s - 1)
                    for k in range(KT):
                        w = ffw[par][:, k // 2, k % 2, :, m, ft * P:(ft + 1) * P]
                        ins = three(B[2 * m + ft % 2][:, :], w[:, 0, :], w[:, 1, :],
                                    h2hi[:, k, bass.ds(t * GT, GT)], h2lo[:, k, bass.ds(t * GT, GT)],
                                    k == 0, k == KT - 1)
                    ins.then_inc(sem_out, 1)

            def down(s, par, tile_no, ft, first_tile=False):
                pe.wait_ge(zhi_done, s + 1)
                pe.wait_ge(zlo_done, s + 1)
                for q in range(GC):
                    if ft == 0 and not first_tile:
                        pe.wait_ge(acc_done, tile_no * GC + (q + 1 - GC))
                    z = zhl[:, ft % 2, :, q * P:(q + 1) * P]
                    w = ffw[par][:, ft // 2, ft % 2, :, 2, :]
                    ins = three(B[4 + q][:, :], z[:, 0, :], z[:, 1, :], w[:, 0, :], w[:, 1, :], ft == 0, ft == FT - 1)
                    ins.then_inc(dn_mm, 1)

            def weights_ready(c, missing):
                pe.wait_ge(whi_done, c * UNITS + (UNITS - missing))
                pe.wait_ge(wlo_done, c * UNITS + (UNITS - missing))

            def chunk(c, par, first=False):
                weights_ready(c, 1)
                s0 = c * STEPS
                for ft in range(FT):
                    if ft == 1:
                        weights_ready(c, 0)
                    if first and ft == 0:
                        pe.wait_ge(hhi_done[1], GC)
                        pe.wait_ge(hlo_done[1], GC)
                    gate_up(c, par, 0, ft, first and ft < 2)
                    if first and ft == 0:
                        ln2(NCH - 2, 0)
                        out_proj(NCH - 1)
                    elif first and ft == 1:
                        ln2(NCH - 1, 1)
                        pe.wait_ge(hm_done[1], NCH)
                        down(s0, par, 0, 0, first_tile=True)
                    elif ft == 0:
                        down(s0 - 1, 1 - par, c * NT - 1, FT - 1)
                    else:
                        down(s0 + ft - 1, par, c * NT, ft - 1)
                if first:
                    pe.wait_ge(hhi_done[1], NCH)
                    pe.wait_ge(hlo_done[1], NCH)
                with pe.Fori(1, NT) as t:
                    for ft in range(FT):
                        gate_up(c, par, t, ft, False)
                        s = s0 + t * FT + ft
                        if ft == 0:
                            down(s - 1, par, c * NT + t - 1, FT - 1)
                        else:
                            down(s - 1, par, c * NT + t, ft - 1)

            chunk(0, 0, first=True)
            with pe.Fori(0, (NF - 2) // 2) as cp:
                chunk(cp * 2 + 1, 1)
                chunk(cp * 2 + 2, 0)
            chunk(NF - 1, 1)
            down(NF * STEPS - 1, 1, NF * NT - 1, FT - 1)


def kernel(**inputs):
    import numpy as np
    import concourse.bacc as bacc
    from concourse.bass_utils import run_bass_kernel_spmd

    a = {name: np.asarray(v) for name, v in inputs.items()}

    def up_codes(w):
        w = w.reshape(NF, 2, P, 2, 2, P)
        return w.transpose(0, 4, 5, 1, 3, 2).reshape(NF, 2, P, FC)

    def up_scales(s):
        s = s.reshape(NF, 2, P, 2, 2, 8)
        return s.transpose(0, 4, 5, 1, 3, 2).reshape(NF, 2, 8, FC)

    codes = np.stack([up_codes(a["L0_ffn_gate_W_packed"]), up_codes(a["L0_ffn_up_W_packed"]),
                      a["L0_ffn_down_W_packed"].reshape(D, NF, 2, P).transpose(1, 2, 3, 0)], axis=3)
    scales = np.stack([up_scales(a["L0_ffn_gate_scales"]), up_scales(a["L0_ffn_up_scales"]),
                       a["L0_ffn_down_scales"].reshape(D, NF, 2, 8).transpose(1, 2, 3, 0)], axis=3)
    arrays = {
        "x": a["L0_attn_x"].reshape(N, D), "wmod": a["L0_wmod"], "cond": a["L0_c"].reshape(KT, P).T,
        "wqkv": a["L0_attn_Wqkv"], "bqkv": a["L0_attn_bqkv"],
        "bqk_cols": a["L0_attn_bqkv"][0:2 * D].reshape(2 * KT, P).T, "wout": a["L0_attn_Wout"],
        "bout": a["L0_attn_bout"], "slopes": a["L0_attn_slopes"],
        "slopes_rg": a["L0_attn_slopes"].reshape(KT, R).T, "codes": codes, "scales": scales,
    }
    arrays = {name: np.ascontiguousarray(v) for name, v in arrays.items()}
    nc = bacc.Bacc("TRN2", target_bir_lowering=False, num_devices=1)
    aps = {name: nc.dram_tensor(name, v.shape, mybir.dt.from_np(v.dtype), kind="ExternalInput").ap()
           for name, v in arrays.items()}
    out = nc.dram_tensor("out", (N, D), F32, kind="ExternalOutput").ap()
    adaln_block_kernel(nc, out=out, **aps)
    r = run_bass_kernel_spmd(nc, [arrays], core_ids=[0])
    return r.results[0]["out"].reshape(1, N, D)
```
